# Optimizing a Trainium2 kernel written in Bass

```python
import numpy as np
import jax
import jax.numpy as jnp

def _softmax(x, axis=-1):
    return jax.nn.softmax(x, axis=axis)

def _gelu(x):
    return jax.nn.gelu(x, approximate=True)

def _silu(x):
    return jax.nn.silu(x)

def _sigmoid(x):
    return jax.nn.sigmoid(x)

def _layernorm(x, axis=-1, eps=1e-05):
    m = jnp.mean(x, axis=axis, keepdims=True)
    v = jnp.var(x, axis=axis, keepdims=True)
    return (x - m) / jnp.sqrt(v + eps)

def _scatter_add(tgt, idx, src, axis=0):
    return tgt.at[idx].add(src)

def _segment_sum(src, seg, n):
    return jax.ops.segment_sum(src, seg, n)
kernel_name = 'mk_decoder_postln_d1_seqx_r4_3c1b0a'

def setup_inputs(seed: int=0):
    np.random.seed(seed)
    _w = jnp.asarray

    def _rec_inputs():
        import jax
        import jax.numpy as jnp
        _rk = jax.random.key(seed)
        x = -0.0003929 + 0.9999 * jax.random.normal(jax.random.fold_in(_rk, 1), (16, 256, 256), jnp.float32)
        _lenS = 256 - jax.random.randint(jax.random.fold_in(_rk, 7), (16,), 0, max(1, 256 // 4) + 1, jnp.int32)
        _lenS2 = 256 - jax.random.randint(jax.random.fold_in(_rk, 8), (16,), 0, max(1, 256 // 4) + 1, jnp.int32)
        _ctx_1024P = jax.random.normal(jax.random.fold_in(_rk, 11), (16, 16, 256), jnp.float32)
        _ctx_1024c = jax.random.dirichlet(jax.random.fold_in(_rk, 511), 0.3 * jnp.ones((16,), jnp.float32), (16, 256))
        _ctx_1024t = jnp.einsum('bsk,bkd->bsd', _ctx_1024c, _ctx_1024P)
        _ctx_1024t = _ctx_1024t * jax.lax.rsqrt(jnp.mean(jnp.square(_ctx_1024t)) + 1e-12) * 0.953939
        ctx_1024 = 2.81802e-05 + 1.00001 * (_ctx_1024t + 0.3 * jax.random.normal(jax.random.fold_in(_rk, 611), (16, 256, 256), jnp.float32))
        return (x, ctx_1024)
    x, ctx_1024 = _rec_inputs()

    def _L0_attn_setup():
        import jax, jax.numpy as jnp
        import numpy as np
        BASE_THETA = 0.5
        K_DOP = 0.2
        K_NOR = 0.15
        K_SERO = 0.1
        DIM = 256
        key = jax.random.key(seed)
        ks = jax.random.split(key, 9)
        scale = 1.0 / np.sqrt(DIM)
        x = jax.random.normal(ks[0], (2, 512, DIM), dtype=jnp.float32)
        Wq = jax.random.normal(ks[1], (DIM, DIM), dtype=jnp.float32) * scale
        bq = jnp.zeros((DIM,), dtype=jnp.float32)
        Wk = jax.random.normal(ks[2], (DIM, DIM), dtype=jnp.float32) * scale
        bk = jnp.zeros((DIM,), dtype=jnp.float32)
        Wv = jax.random.normal(ks[3], (DIM, DIM), dtype=jnp.float32) * scale
        bv = jnp.zeros((DIM,), dtype=jnp.float32)
        Wo = jax.random.normal(ks[4], (DIM, DIM), dtype=jnp.float32) * scale
        bo = jnp.zeros((DIM,), dtype=jnp.float32)
        return {'x': x, 'Wq': Wq, 'bq': bq, 'Wk': Wk, 'bk': bk, 'Wv': Wv, 'bv': bv, 'Wo': Wo, 'bo': bo}
    _L0_attn_all = _L0_attn_setup()
    _L0_attn_in = {k: v for k, v in _L0_attn_all.items() if k in ('Wq', 'bq', 'Wk', 'bk', 'Wv', 'bv', 'Wo', 'bo')}
    del _L0_attn_all

    def _L0_xattn_setup():
        import jax, jax.numpy as jnp
        import numpy as np
        B, S, E, H = (4, 1024, 256, 16)
        rng = jax.random.key(seed)
        ks = jax.random.split(rng, 7)
        s = 0.02
        return {'query': jax.random.normal(ks[0], (B, S, E), jnp.float32), 'key': jax.random.normal(ks[1], (B, S, E), jnp.float32), 'value': jax.random.normal(ks[2], (B, S, E), jnp.float32), 'in_proj_w': jax.random.normal(ks[3], (3 * E, E), jnp.float32) * s, 'in_proj_b': jax.random.normal(ks[4], (3 * E,), jnp.float32) * s, 'out_proj_w': jax.random.normal(ks[5], (E, E), jnp.float32) * s, 'out_proj_b': jax.random.normal(ks[6], (E,), jnp.float32) * s, 'chunk_size': 64}
    _L0_xattn_all = _L0_xattn_setup()
    _L0_xattn_in = {k: v for k, v in _L0_xattn_all.items() if k in ('in_proj_w', 'in_proj_b', 'out_proj_w', 'out_proj_b')}
    del _L0_xattn_all

    def _L0_ffn_setup():
        import jax, jax.numpy as jnp
        import numpy as np
        from jax import lax
        B, S, H = (2, 256, 256)
        I = 128
        E = 32
        TOP_K = 4
        N_GROUP = 4
        TOPK_GROUP = 2
        SCALE = 2.5
        N_SHARED = 2
        SH_I = I * N_SHARED

        def _route(tokens, router_weight, router_bias):
            logits = tokens.astype(jnp.float32) @ router_weight.astype(jnp.float32).T
            scores = jax.nn.sigmoid(logits)
            sfc = scores + router_bias[None, :]
            T = tokens.shape[0]
            grp = sfc.reshape(T, N_GROUP, E // N_GROUP)
            group_scores = lax.top_k(grp, 2)[0].sum(-1)
            _, gidx = lax.top_k(group_scores, TOPK_GROUP)
            gmask = jax.nn.one_hot(gidx, N_GROUP, dtype=sfc.dtype).sum(1)
            smask = jnp.broadcast_to(gmask[:, :, None], (T, N_GROUP, E // N_GROUP)).reshape(T, E)
            tmp = jnp.where(smask > 0, sfc, 0.0)
            _, topk_idx = lax.top_k(tmp, TOP_K)
            topk_w = jnp.take_along_axis(scores, topk_idx, axis=1)
            topk_w = topk_w / (topk_w.sum(-1, keepdims=True) + 1e-20)
            topk_w = topk_w * SCALE
            return (topk_idx, topk_w)
        key = jax.random.key(seed)
        ks = jax.random.split(key, 10)
        std = 0.02
        return {'hidden_states': jax.random.normal(ks[0], (B, S, H), jnp.float32), 'router_weight': jax.random.normal(ks[1], (E, H), jnp.float32) * std, 'router_bias': jnp.zeros((E,), jnp.float32), 'gate_w': jax.random.normal(ks[2], (E, I, H), jnp.float32) * std, 'up_w': jax.random.normal(ks[3], (E, I, H), jnp.float32) * std, 'down_w': jax.random.normal(ks[4], (E, H, I), jnp.float32) * std, 'shared_gate_w': jax.random.normal(ks[5], (SH_I, H), jnp.float32) * std, 'shared_up_w': jax.random.normal(ks[6], (SH_I, H), jnp.float32) * std, 'shared_down_w': jax.random.normal(ks[7], (H, SH_I), jnp.float32) * std}
    _L0_ffn_all = _L0_ffn_setup()
    _L0_ffn_in = {k: v for k, v in _L0_ffn_all.items() if k in ('router_weight', 'router_bias', 'gate_w', 'up_w', 'down_w', 'shared_gate_w', 'shared_up_w', 'shared_down_w')}
    del _L0_ffn_all
    return {'x': x, 'ctx_1024': ctx_1024, 'L0_attn_Wq': _L0_attn_in['Wq'], 'L0_attn_bq': _L0_attn_in['bq'], 'L0_attn_Wk': _L0_attn_in['Wk'], 'L0_attn_bk': _L0_attn_in['bk'], 'L0_attn_Wv': _L0_attn_in['Wv'], 'L0_attn_bv': _L0_attn_in['bv'], 'L0_attn_Wo': _L0_attn_in['Wo'], 'L0_attn_bo': _L0_attn_in['bo'], 'L0_xattn_in_proj_w': _L0_xattn_in['in_proj_w'], 'L0_xattn_in_proj_b': _L0_xattn_in['in_proj_b'], 'L0_xattn_out_proj_w': _L0_xattn_in['out_proj_w'], 'L0_xattn_out_proj_b': _L0_xattn_in['out_proj_b'], 'L0_ffn_router_weight': _L0_ffn_in['router_weight'], 'L0_ffn_router_bias': _L0_ffn_in['router_bias'], 'L0_ffn_gate_w': _L0_ffn_in['gate_w'], 'L0_ffn_up_w': _L0_ffn_in['up_w'], 'L0_ffn_down_w': _L0_ffn_in['down_w'], 'L0_ffn_shared_gate_w': _L0_ffn_in['shared_gate_w'], 'L0_ffn_shared_up_w': _L0_ffn_in['shared_up_w'], 'L0_ffn_shared_down_w': _L0_ffn_in['shared_down_w']}

def reference(x, ctx_1024, L0_attn_Wq, L0_attn_bq, L0_attn_Wk, L0_attn_bk, L0_attn_Wv, L0_attn_bv, L0_attn_Wo, L0_attn_bo, L0_xattn_in_proj_w, L0_xattn_in_proj_b, L0_xattn_out_proj_w, L0_xattn_out_proj_b, L0_ffn_router_weight, L0_ffn_router_bias, L0_ffn_gate_w, L0_ffn_up_w, L0_ffn_down_w, L0_ffn_shared_gate_w, L0_ffn_shared_up_w, L0_ffn_shared_down_w):
    import jax
    import jax.numpy as jnp

    def _L0_attn_ref(x, Wq, bq, Wk, bk, Wv, bv, Wo, bo):
        import jax, jax.numpy as jnp
        import numpy as np
        BASE_THETA = 0.5
        K_DOP = 0.2
        K_NOR = 0.15
        K_SERO = 0.1
        DIM = 256
        q = jnp.einsum('bsd,ed->bse', x, Wq) + bq
        k = jnp.einsum('bsd,ed->bse', x, Wk) + bk
        v = jnp.einsum('bsd,ed->bse', x, Wv) + bv
        qk = jnp.einsum('bsd,btd->bst', q, k)
        theta = BASE_THETA + K_DOP * jax.nn.sigmoid(qk) + K_NOR * jnp.tanh(qk) + K_SERO * jax.nn.relu(qk)
        attn = jax.nn.softmax(theta, axis=-1)
        out = jnp.einsum('bst,btd->bsd', attn, v)
        return jnp.einsum('bsd,ed->bse', out, Wo) + bo

    def _L0_xattn_ref(query, key, value, in_proj_w, in_proj_b, out_proj_w, out_proj_b, chunk_size):
        import jax, jax.numpy as jnp
        import numpy as np
        B, S, E, H = (4, 1024, 256, 16)
        b, seq, e = query.shape
        h = H
        hd = e // h
        n = seq // chunk_size
        wq, wk, wv = jnp.split(in_proj_w, 3, axis=0)
        bq, bk, bv = jnp.split(in_proj_b, 3)
        q = query @ wq.T + bq
        k = key @ wk.T + bk
        v = value @ wv.T + bv

        def to_blocks(x):
            return x.reshape(b, n, chunk_size, h, hd)
        qh, kh, vh = (to_blocks(q), to_blocks(k), to_blocks(v))
        scores = jnp.einsum('bnqhd,bnkhd->bnhqk', qh, kh) / np.sqrt(hd)
        attn = jax.nn.softmax(scores, axis=-1)
        out = jnp.einsum('bnhqk,bnkhd->bnqhd', attn, vh).reshape(b, seq, e)
        return out @ out_proj_w.T + out_proj_b

    def _L0_ffn_ref(hidden_states, router_weight, router_bias, gate_w, up_w, down_w, shared_gate_w, shared_up_w, shared_down_w):
        import jax, jax.numpy as jnp
        import numpy as np
        from jax import lax
        B, S, H = (2, 256, 256)
        I = 128
        E = 32
        TOP_K = 4
        N_GROUP = 4
        TOPK_GROUP = 2
        SCALE = 2.5
        N_SHARED = 2
        SH_I = I * N_SHARED

        def _route(tokens, router_weight, router_bias):
            logits = tokens.astype(jnp.float32) @ router_weight.astype(jnp.float32).T
            scores = jax.nn.sigmoid(logits)
            sfc = scores + router_bias[None, :]
            T = tokens.shape[0]
            grp = sfc.reshape(T, N_GROUP, E // N_GROUP)
            group_scores = lax.top_k(grp, 2)[0].sum(-1)
            _, gidx = lax.top_k(group_scores, TOPK_GROUP)
            gmask = jax.nn.one_hot(gidx, N_GROUP, dtype=sfc.dtype).sum(1)
            smask = jnp.broadcast_to(gmask[:, :, None], (T, N_GROUP, E // N_GROUP)).reshape(T, E)
            tmp = jnp.where(smask > 0, sfc, 0.0)
            _, topk_idx = lax.top_k(tmp, TOP_K)
            topk_w = jnp.take_along_axis(scores, topk_idx, axis=1)
            topk_w = topk_w / (topk_w.sum(-1, keepdims=True) + 1e-20)
            topk_w = topk_w * SCALE
            return (topk_idx, topk_w)
        tokens = hidden_states.reshape(-1, H)
        topk_idx, topk_w = _route(tokens, router_weight, router_bias)
        gate_vals = jax.nn.silu(jnp.einsum('th,eih->tei', tokens, gate_w))
        up_vals = jnp.einsum('th,eih->tei', tokens, up_w)
        hidden_vals = gate_vals * up_vals
        expert_out = jnp.einsum('tei,ehi->teh', hidden_vals, down_w)
        sel = jnp.take_along_axis(expert_out, topk_idx[:, :, None], axis=1)
        mixed = (sel * topk_w[:, :, None].astype(sel.dtype)).sum(1)
        mixed = mixed.reshape(hidden_states.shape)
        sg = jax.nn.silu(jnp.einsum('bsh,ih->bsi', hidden_states, shared_gate_w))
        su = jnp.einsum('bsh,ih->bsi', hidden_states, shared_up_w)
        shared = jnp.einsum('bsi,hi->bsh', sg * su, shared_down_w)
        return mixed + shared
    x = _layernorm(x + _L0_attn_ref(x, L0_attn_Wq, L0_attn_bq, L0_attn_Wk, L0_attn_bk, L0_attn_Wv, L0_attn_bv, L0_attn_Wo, L0_attn_bo), axis=-1)
    x = _layernorm(x + _L0_xattn_ref(x, ctx_1024, ctx_1024, L0_xattn_in_proj_w, L0_xattn_in_proj_b, L0_xattn_out_proj_w, L0_xattn_out_proj_b, 64), axis=-1)
    x = _layernorm(x + _L0_ffn_ref(x, L0_ffn_router_weight, L0_ffn_router_bias, L0_ffn_gate_w, L0_ffn_up_w, L0_ffn_down_w, L0_ffn_shared_gate_w, L0_ffn_shared_up_w, L0_ffn_shared_down_w), axis=-1)
    return x

_drawn_inputs = setup_inputs


def setup_inputs(seed=0):
    import zlib

    import numpy as np

    out = dict(_drawn_inputs(seed))
    spreads = {'L0_attn_bq': (0.0, 0.3),
     'L0_attn_bk': (0.0, 0.8),
     'L0_attn_bv': (0.0, 0.1),
     'L0_attn_bo': (0.0, 0.1),
     'L0_ffn_router_bias': (0.0, 0.503)}
    factors = {'L0_xattn_in_proj_b': 8.0,
     'L0_xattn_out_proj_b': 2.713,
     'L0_ffn_router_weight': 4.6,
     'L0_ffn_gate_w': 3.805,
     'L0_ffn_up_w': 3.755,
     'L0_ffn_down_w': 3.759,
     'L0_ffn_shared_gate_w': 3.382,
     'L0_ffn_shared_up_w': 3.322,
     'L0_ffn_shared_down_w': 3.325}
    for name, (base, spread) in spreads.items():
        noise = np.random.default_rng([zlib.crc32(name.encode()), seed]).standard_normal(out[name].shape)
        drawn = base * np.exp(spread * noise) if base else spread * noise
        out[name] = jnp.asarray(drawn.astype(out[name].dtype))
    for name, factor in factors.items():
        out[name] = (out[name] * factor).astype(out[name].dtype)
    return out
```

```python
import numpy as np
import concourse.bass as bass
from concourse import mybir
from contextlib import ExitStack

P = 128
D = 256
DK = D // P
S = 256
T = S // P
H, HD = 16, 16
CH = 64
NP = H // 2
E, EI = 32, 128
GRP, GE = 4, E // 4
TOPK, TOPG = 4, 2
SH = 256
ROUTE_SCALE = 2.5
LN_EPS = 1e-5
BIG = 1e30

RW = D + E + 1
ACCS = 4
UNROLL = 8
WORD = 5
VW = 2 * HD + 2


def shapes(nseq):
    n = nseq * S
    blocks = n * TOPK // P + E
    blocks = -(-blocks // UNROLL) * UNROLL
    return n, n + P, blocks


def constants(nseq):
    n, region, blocks = shapes(nseq)
    p = np.arange(P)
    table = blocks + UNROLL
    parts = [
        np.eye(P),
        (p[:, None] < p[None, :]),
        np.ones((P, P)),
        (p[:, None] // HD % 2 == np.arange(2)[None]),
        (p[:, None] // CH == np.r_[np.repeat(np.arange(2), HD), np.arange(2)][None]),
        np.tile(np.arange(E) * region + 1.0, (P, 1)),
        (p[:, None] <= np.arange(E)[None]),
        np.tile(np.arange(table), (P, 1)),
    ]
    at, out = 0, {}
    for name, a in zip(("ident", "before", "ones", "headmask", "valmask", "region", "upto", "blockno"), parts):
        out[name] = (at, a.shape[1])
        at += a.shape[1]
    return out, np.concatenate([a.astype(np.float32) for a in parts], axis=1)


def build(nc, d, out):
    F32, I32 = mybir.dt.float32, mybir.dt.int32
    ALU, ACT, AX = mybir.AluOpType, mybir.ActivationFunctionType, mybir.AxisListType
    nseq = d["x"].shape[0]
    N, REGION, BLOCKS = shapes(nseq)
    CC, _ = constants(nseq)
    TABLE = BLOCKS + UNROLL

    routed = nc.dram_tensor("routed", ((E + 1) * REGION, RW), F32).ap()
    accs = [nc.dram_tensor(f"acc{a}", (N + P, D), F32).ap() for a in range(ACCS)]

    ctx = ExitStack()
    with ctx:
        def sb(name, shape, dt=F32):
            return ctx.enter_context(nc.sbuf_tensor(f"{name}_tile", shape, dt))

        def sem(name):
            return ctx.enter_context(nc.semaphore(name))

        bank = [ctx.enter_context(nc.psum_tensor(f"bank{b}", [P, 512], F32)) for b in range(8)]

        const = sb("const", [P, sum(w for _, w in CC.values())])

        def c(name, rows=P):
            at, w = CC[name]
            return const[0:rows, at:at + w]

        ident = c("ident")
        w_attn = sb("w_attn", [P, DK, 4, D])
        b_attn = sb("b_attn", [P, DK, 4])
        b_cross = sb("b_cross", [P, DK, 2])
        bo_rows = sb("bo_rows", [1, 2, D])
        w_cross = sb("w_cross", [P, DK, 4, D])
        w_router = sb("w_router", [P, DK, E])
        bias_router = sb("bias_router", [P, E])
        w_shared_in = sb("w_shared_in", [P, DK, 2 * SH])
        w_shared_out = sb("w_shared_out", [P, DK, D])
        w_expert = sb("w_expert", [P, E, 3 * D])
        w_flat = w_expert[:, :, :].rearrange("p e n -> p (e n)")
        rep = w_flat[:, 0:DK * 3 * P].rearrange("p (k j n) -> p k j n", k=DK, j=3)
        g_qk = sb("g_qk", [P, DK, D])
        g_vo = sb("g_vo", [P, DK, D])
        g_bias = sb("g_bias", [P, DK, 2])
        c_bqbk = sb("c_bqbk", [P, 1])
        c_out = sb("c_out", [P, 2, D])

        pad = sb("pad", [P, RW])
        counts = sb("counts", [E, 1])
        cnt_i = sb("cnt_i", [E, 1], I32)
        nblk = sb("nblk", [E, 1])
        upto = sb("upto", [E, 1])
        padrow = sb("padrow", [1, E], I32)
        FT = min(2, N // (2 * P))
        fhalf = sb("fhalf", [P, FT])
        pad_id = sb("pad_id", [P, 1], I32)
        tok_id = sb("tok_id", [P, T], I32)
        macc = sb("macc", [P, E])

        ctx_a = ExitStack()

        def sa(name, shape, dt=F32):
            return ctx_a.enter_context(nc.sbuf_tensor(f"{name}_tile", shape, dt))

        x_sb = sa("x_sb", [P, T, D])
        xT = sa("xT", [P, DK, S])
        cT = sa("cT", [P, DK, S // CH, 2, CH])
        zT = sa("zT", [P, DK, S])
        vo = sa("vo", [P, T, D])
        r_sb = sa("r_sb", [P, T])
        r_half = sa("r_half", [P, T])
        r_neg = sa("r_neg", [P, T])
        t1 = sa("t1", [P, T, S])
        t2 = sa("t2", [P, T, S])
        th = sa("th", [P, T, S])
        mx = sa("mx", [P, T])
        nmx = sa("nmx", [P, T])
        pr = sa("pr", [P, T, S])
        den = sa("den", [P, T])
        prT = sa("prT", [P, T, T, P])
        xc = sa("xc", [P, T, D])
        st1 = sa("st1", [P, T, 6])
        ag1 = sa("ag1", [P, T, 2])
        ve1 = sa("ve1", [P, T])
        rs1 = sa("rs1", [P, T])
        x1 = sa("x1", [P, T, D])
        x1T = sa("x1T", [P, DK, S])
        half_neg = sa("half_neg", [P, T])
        qT = sa("qT", [P, DK, S])
        kM = sa("kM", [P, DK, S // CH, 2, CH])
        vM = sa("vM", [P, S // CH, NP, VW])
        mxh = sa("mxh", [P, 4, T, 2, 2])
        sh = sa("sh", [P, 4, T, 4 * CH])
        pT = sa("pT", [P, T, NP, P])
        rden = sa("rden", [P, T, NP, 2])
        o_sb = sa("o_sb", [P, T, D])
        oT = sa("oT", [P, DK, S])
        xc2 = sa("xc2", [P, T, D])
        st2 = sa("st2", [P, T, 6])
        ag2 = sa("ag2", [P, T, 2])
        ve2 = sa("ve2", [P, T])
        rs2 = sa("rs2", [P, T])
        row = sa("row", [P, T, RW])
        x2T = sa("x2T", [P, DK, S])
        gt = sa("gt", [P, T, SH])
        hs = sa("hs", [P, T, SH])
        hsT = sa("hsT", [P, DK, S])
        acc_sb = sa("acc_sb", [P, T, D])
        sc = sa("sc", [P, T, E])
        sfc = sa("sfc", [P, T, E])
        g8 = sa("g8", [P, T, GRP, 8])
        gs = sa("gs", [P, T, GRP + 6])
        gm = sa("gm", [P, T, 8])
        gv = sa("gv", [P, T, 8])
        gr = sa("gr", [P, T, GRP + 6])
        gsel = sa("gsel", [P, T, GRP])
        tmp = sa("tmp", [P, T, E + 4])
        em = sa("em", [P, T, 8])
        ev = sa("ev", [P, T, 8])
        er = sa("er", [P, T, E + 4])
        msel = sa("msel", [P, T, E])
        wsum = sa("wsum", [P, T])
        wraw = sa("wraw", [P, T, E])
        key = sa("key", [P, T, E])
        slot = sa("slot", [P, T, 8])
        idx = sa("idx", [P, T, TOPK], I32)

        ctx_a.close()

        past = sb("past", [E, TABLE])
        tab = sb("tab", [1, 2, TABLE])
        tab_i = sb("tab_i", [1, 2, TABLE], I32)
        words = sb("words", [1, BLOCKS // UNROLL, 2], I32)
        rowsb = [sb(f"rowsb{u}", [P, RW]) for u in range(UNROLL)]
        xbT = [sb(f"xbT{u}", [P, D]) for u in range(2)]
        wcol = [sb(f"wcol{u}", [P, 1]) for u in range(2)]
        gb = [sb(f"gb{u}", [P, EI]) for u in range(2)]
        hb1 = [sb(f"hb1_{u}", [P, EI]) for u in range(2)]
        hb = [sb(f"hb{u}", [P, EI]) for u in range(2)]
        hbT = [sb(f"hbT{u}", [P, EI]) for u in range(2)]
        yb = [sb(f"yb{u}", [P, D]) for u in range(ACCS)]

        fa = [sb(f"fa{u}", [P, ACCS, FT, D]) for u in range(2)]
        fs = [sb(f"fs{u}", [P, FT, D]) for u in range(2)]
        fo = [sb(f"fo{u}", [P, FT, D]) for u in range(2)]
        fst = [sb(f"fst{u}", [P, FT, 6]) for u in range(2)]
        fag = [sb(f"fag{u}", [P, FT, 2]) for u in range(2)]
        fmean = [sb(f"fmean{u}", [P, FT]) for u in range(2)]
        fve = [sb(f"fve{u}", [P, FT]) for u in range(2)]
        frs = [sb(f"frs{u}", [P, FT]) for u in range(2)]

        names = {}

        def S_(name):
            if name not in names:
                names[name] = sem(name)
            return names[name]

        class Chain:

            def __init__(self, eng, name, base):
                self.eng, self.name, self.sem, self.base, self.n = eng, name, S_(name), base, 0

            def __call__(self, ins, alone=False):
                self.n += 1
                ins.then_inc(self.sem, 1)
                if alone:
                    wait_apart(self.eng, (self.name, self.base + self.n))
                else:
                    self.eng.wait_ge(self.sem, self.base + self.n)

        FIRST = 2
        LOOKED_BACK = (
            "v_x1T", "v_pre1", "v_th", "a_tanh", "v_hs", "a_hsT", "v_acc", "v_key", "p_s1", "p_prT", "p_av1", "p_s2",
            "p_av2", "p_out2", "p_shin", "v_msel", "p_shout", "a_pr", "p_x1T", "g_xc2", "p_q", "p_pT", "p_oT",
            "p_rank", "p_hsT", "v_x1", "v_x2", "st_acc",
            "a_xbT", "v_hb", "a_yb", "p_gu", "p_hbT", "p_down",
            *(f"{n}{u}" for n in ("v_f", "v_o", "st_out") for u in range(2)))
        STARTED = ("st_row", *(f"st_acc{a}" for a in range(ACCS)))

        def wait(e, name, value):
            if not isinstance(value, int) or value > 0:
                e.wait_ge(S_(name), value + (FIRST if name in LOOKED_BACK else 16 if name in STARTED else 0))

        def wait_apart(e, *waits):
            for name, value in waits:
                wait(e, name, value)
                e.nop().then_inc(S_("apart"), 1)

        def number(turn, u):
            return turn * UNROLL + u

        def loads_of_buffer(turn, u):
            return turn + (u // UNROLL + 1)

        def adds_before(turn, u):
            return turn * (UNROLL // ACCS) + u // ACCS

        def experts(e, turn):
            out = []
            for j in range(2):
                w = e.value_load(words[0:1, bass.ds(turn, 1), j], min_val=0, max_val=E ** WORD - 1)
                out += [w // E ** v % E for v in range(WORD)]
            return out

        blk = ctx.enter_context(nc.Block())

        def pe_setup(e):
            wait(e, "ld_const", 16 * 7)
            for db in range(DK):
                for k in range(DK):
                    e.matmul(bank[0][:, db * D:(db + 1) * D], w_attn[:, k, 0, db * P:(db + 1) * P],
                             w_attn[:, k, 1, :], start=k == 0, stop=k == DK - 1)
            for db in range(DK):
                for k in range(DK):
                    e.matmul(bank[1][:, db * D:(db + 1) * D], w_attn[:, k, 2, db * P:(db + 1) * P],
                             w_attn[:, k, 3, :], start=k == 0, stop=k == DK - 1)
            for j in range(2):
                for db in range(DK):
                    for k in range(DK):
                        e.matmul(bank[2][:, 2 * j + db:2 * j + db + 1], w_attn[:, k, 1 - j, db * P:(db + 1) * P],
                                 b_attn[:, k, j:j + 1], start=k == 0, stop=k == DK - 1)
            wait(e, "v_rep", 1)
            for k in range(DK):
                e.matmul(bank[2][:, 8:9], rep[:, k, 0, :], b_attn[:, k, 1:2], start=k == 0, stop=k == DK - 1)
            for j, (w, wi) in enumerate(((w_attn, 3), (w_cross, 3))):
                for k in range(DK):
                    e.matmul(bank[3][:, j * D:(j + 1) * D], rep[:, k, 1 + j, :], w[:, k, wi, :],
                             start=k == 0, stop=False)
                m = e.matmul(bank[3][:, j * D:(j + 1) * D], c("ones", 1), bo_rows[:, j, :], start=False, stop=True)
            m.then_inc(S_("p_setup"), 1)
            wait(e, "v_setup", 1)

        def pe_z(e, i):
            wait(e, "ld_xT", 16 * (i + 1))
            wait(e, "v_x1T", i)
            for db in range(DK):
                for k in range(DK):
                    m = e.matmul(bank[0][:, db * S:(db + 1) * S], g_qk[:, k, db * P:(db + 1) * P], xT[:, k, :],
                                 start=k == 0, stop=k == DK - 1)
            m.then_inc(S_("p_z"), 1)
            wait(e, "v_pre1", i)
            for t in range(T):
                for k in range(DK):
                    m = e.matmul(bank[1][:, t * D:(t + 1) * D], xT[:, k, t * P:(t + 1) * P], g_vo[:, k, :],
                                 start=k == 0, stop=k == DK - 1)
            m.then_inc(S_("p_vo"), 1)
            wait(e, "v_th", i)
            wait(e, "a_tanh", i)
            for t in range(T):
                for k in range(DK):
                    m = e.matmul(bank[2][:, t:t + 1], xT[:, k, t * P:(t + 1) * P], g_bias[:, k, 1:2],
                                 start=k == 0, stop=k == DK - 1)
            m.then_inc(S_("p_r"), 1)

        def pe_scores1(e, i):
            wait(e, "a_z", i + 1)
            wait(e, "v_r", i + 1)
            for t in range(T):
                for k in range(DK):
                    m = e.matmul(bank[2][:, t * S:(t + 1) * S], zT[:, k, t * P:(t + 1) * P], xT[:, k, :],
                                 start=k == 0, stop=k == DK - 1)
            m.then_inc(S_("p_s1"), 1)

        def pe_prT(e, i):
            wait(e, "a_pr", i + 1)
            for t in range(T):
                for u in range(T):
                    m = e.transpose(bank[0][:, (t * T + u) * P:(t * T + u + 1) * P],
                                    pr[:, t, u * P:(u + 1) * P], ident)
            m.then_inc(S_("p_prT"), 1)

        def pe_av1(e, i):
            wait(e, "a_prT", i + 1)
            wait(e, "a_vo", i + 1)
            for t in range(T):
                for u in range(T):
                    m = e.matmul(bank[1][:, t * D:(t + 1) * D], prT[:, t, u, :], vo[:, u, :],
                                 start=u == 0, stop=u == T - 1)
            m.then_inc(S_("p_av1"), 1)

        def pe_x1T(e, i):
            wait(e, "v_x1", i + 1)
            for k in range(DK):
                for t in range(T):
                    m = e.transpose(bank[0][:, k * S + t * P:k * S + (t + 1) * P],
                                    x1[:, t, k * P:(k + 1) * P], ident)
            m.then_inc(S_("p_x1T"), 1)

        def pe_kv(e, i):
            wait(e, "ld_cT", 16 * (i + 1))
            wait(e, "v_hs", i)
            for db in range(DK):
                for k in range(DK):
                    m = e.matmul(bank[3][:, db * S:(db + 1) * S], w_cross[:, k, 1, db * P:(db + 1) * P],
                                 cT[:, k, :, 0, :],
                                 start=k == 0, stop=k == DK - 1)
            m.then_inc(S_("p_k"), 1)
            wait(e, "a_hsT", i)
            for ch in range(S // CH):
                b, at = 4 + ch // 2, ch % 2 * D
                for k in range(DK):
                    m = e.matmul(bank[b][:, at:at + D], cT[:, k, ch, :, :].rearrange("p a c -> p (a c)"), w_cross[:, k, 2, :],
                                 start=k == 0, stop=k == DK - 1)
            m.then_inc(S_("p_v"), 1)

        def pe_q(e, i):
            wait(e, "v_x1T", i + 1)
            wait(e, "v_acc", i)
            for db in range(DK):
                for k in range(DK):
                    m = e.matmul(bank[6][:, db * S:(db + 1) * S], w_cross[:, k, 0, db * P:(db + 1) * P], x1T[:, k, :],
                                 start=k == 0, stop=k == DK - 1)
            m.then_inc(S_("p_q"), 1)

        def pe_scores2(e, i):
            wait(e, "a_q", i + 1)
            wait(e, "v_k", i + 1)
            wait(e, "v_v", i + 1)
            for t in range(T):
                for hf in range(DK):
                    for a in range(2):
                        for j in range(4):
                            ch, rows = 2 * t + a, slice(32 * j, 32 * j + 32)
                            at = (t * DK + hf) * 2 * CH
                            m = e.matmul(bank[3 + j][a * CH:(a + 1) * CH, at:at + 2 * CH],
                                         qT[rows, hf, ch * CH:(ch + 1) * CH],
                                         kM[rows, hf, ch, :, :], start=True, stop=True)
            m.then_inc(S_("p_s2"), 1)

        def pe_pT(e, i):
            wait(e, "a_sh", i + 1)
            for t in range(T):
                for hf in range(DK):
                    for j in range(4):
                        m = e.transpose(bank[3 + 2 * t + hf][:, j * P:(j + 1) * P],
                                        sh[:, j, t, hf * P:(hf + 1) * P], ident)
                    m.then_inc(S_("p_pT"), 1)

        def pe_av2(e, i):
            wait(e, "v_key", i)
            for t in range(T):
                wait(e, "a_pT", 2 * i + t + 1)
                wait(e, "v_pT", 2 * i + t + 1)
                for a in range(2):
                    for j in range(NP):
                        o = bank[7 - 4 * t]
                        m = e.matmul(o[a * CH:(a + 1) * CH, j * VW:(j + 1) * VW],
                                     pT[:, t, j, a * CH:(a + 1) * CH], vM[:, 2 * t + a, j, :],
                                     start=True, stop=True)
                m.then_inc(S_("p_av2"), 1)

        def pe_oT(e, i):
            wait(e, "v_o", i + 1)
            for k in range(DK):
                for t in range(T):
                    m = e.transpose(bank[4][:, k * S + t * P:k * S + (t + 1) * P],
                                    o_sb[:, t, k * P:(k + 1) * P], ident)
            m.then_inc(S_("p_oT"), 1)

        def pe_out2(e, i):
            wait(e, "a_oT", i + 1)
            for t in range(T):
                for k in range(DK):
                    m = e.matmul(bank[5][:, t * D:(t + 1) * D], oT[:, k, t * P:(t + 1) * P], w_cross[:, k, 3, :],
                                 start=k == 0, stop=k == DK - 1)
            m.then_inc(S_("p_out2"), 1)

        def pe_x2T(e, i):
            wait(e, "v_x2", i + 1)
            for k in range(DK):
                for t in range(T):
                    m = e.transpose(bank[6][:, k * S + t * P:k * S + (t + 1) * P],
                                    row[:, t, k * P:(k + 1) * P], ident)
            m.then_inc(S_("p_x2T"), 1)

        def pe_router(e, i):
            wait(e, "a_x2T", i + 1)
            for t in range(T):
                for k in range(DK):
                    m = e.matmul(bank[7][:, t * E:(t + 1) * E], x2T[:, k, t * P:(t + 1) * P], w_router[:, k, :],
                                 start=k == 0, stop=k == DK - 1)
            m.then_inc(S_("p_router"), 1)

        def pe_shared_in(e, i):
            for t in range(T):
                for k in range(DK):
                    m = e.matmul(bank[3 + t][:, :], x2T[:, k, t * P:(t + 1) * P], w_shared_in[:, k, :],
                                 start=k == 0, stop=k == DK - 1)
            m.then_inc(S_("p_shin"), 1)

        def pe_hsT(e, i):
            wait(e, "v_hs", i + 1)
            for k in range(DK):
                for t in range(T):
                    m = e.transpose(bank[5][:, k * S + t * P:k * S + (t + 1) * P],
                                    hs[:, t, k * P:(k + 1) * P], ident)
            m.then_inc(S_("p_hsT"), 1)

        def pe_shared_out(e, i):
            wait(e, "a_hsT", i + 1)
            for t in range(T):
                for k in range(DK):
                    m = e.matmul(bank[6][:, t * D:(t + 1) * D], hsT[:, k, t * P:(t + 1) * P], w_shared_out[:, k, :],
                                 start=k == 0, stop=k == DK - 1)
            m.then_inc(S_("p_shout"), 1)

        def pe_rank(e, i):
            wait(e, "v_msel", i + 1)
            for t in range(T):
                o = bank[7][:, 128 + t * E:128 + (t + 1) * E]
                e.matmul(o, c("before"), msel[:, t, :], start=True, stop=False)
                for u in range(t):
                    e.matmul(o, c("ones"), msel[:, u, :], start=False, stop=False)
                m = e.matmul(o, c("ones"), macc[:, :], start=False, stop=True)
            m.then_inc(S_("p_rank"), 1)

        def pe_tables(e):
            wait(e, "v_key", nseq)
            wait(e, "v_acc", nseq)
            e.matmul(bank[7][0:E, 0:1], macc[:, :], c("ones")[:, 0:1], start=True, stop=True)
            e.matmul(bank[7][0:1, 32:32 + E], c("ones")[:, 0:1], macc[:, :], start=True, stop=True)\
                .then_inc(S_("p_tab"), 1)
            wait(e, "v_nblk", 1)
            e.matmul(bank[7][0:E, 1:2], c("upto", E), nblk[:, :], start=True, stop=True).then_inc(S_("p_tab"), 1)
            wait(e, "v_past", 1)
            e.matmul(bank[6][0:1, 0:TABLE], c("ones", E)[:, 0:1], past[:, :], start=True, stop=True)
            e.matmul(bank[6][0:1, TABLE:2 * TABLE], nblk[:, :], past[:, :], start=True, stop=True)\
                .then_inc(S_("p_tab"), 1)
            wait(e, "v_tab", 1)

        def pe_xbT(e, b, u):
            wait(e, f"ld_row{u % UNROLL}", 16 * loads_of_buffer(b, u))
            n = number(b, u)
            wait(e, "a_xbT", n - 1)
            for k in range(DK):
                m = e.transpose(bank[u % 2][:, k * P:(k + 1) * P], rowsb[u % UNROLL][:, k * P:(k + 1) * P], ident)
            m.then_inc(S_("p_xbT"), 1)

        def pe_gu(e, b, u, w):
            n = number(b, u)
            wait(e, "a_xbT", n + 1)
            wait(e, "v_hb", n - 1)
            for k in range(DK):
                m = e.matmul(bank[2 + u % 2][:, 0:2 * EI], xbT[u % 2][:, k * P:(k + 1) * P],
                             w_flat[:, bass.ds(w * 3 * D + k * D, D)], start=k == 0, stop=k == DK - 1)
            m.then_inc(S_("p_gu"), 1)

        def pe_hbT(e, b, u):
            n = number(b, u)
            wait(e, "v_hb", n + 1)
            e.transpose(bank[4 + u % 2][:, 0:P], hb[u % 2][:, :], ident).then_inc(S_("p_hbT"), 1)

        def pe_down(e, b, u, w):
            n = number(b, u)
            wait(e, "v_hbT", n + 1)
            wait(e, "a_yb", n - 1)
            e.matmul(bank[6 + u % 2][:, 0:D], hbT[u % 2][:, :], w_flat[:, bass.ds(w * 3 * D + 2 * D, D)],
                     start=True, stop=True).then_inc(S_("p_down"), 1)

        def sync_out(e):
            for a in range(ACCS):
                wait(e, f"st_acc{a}", 16 * BLOCKS // ACCS)
            with e.Fori(0, N // (2 * FT * P)) as i:
                for u in range(2):
                    wait(e, f"v_f{u}", i)
                    for a in range(ACCS):
                        e.dma_start(fa[u][:, a, :, :], accs[a][bass.ds((i * 2 + u) * FT * P, FT * P), :].rearrange(
                            "(t p) d -> p t d", p=P)).then_inc(S_(f"ld_f{u}"), 16)

        def vec_out(e):
            with e.Fori(0, N // (2 * FT * P)) as i:
                for u in range(2):
                    ch = Chain(e, f"vo{u}", 4 * i)
                    wait(e, f"ld_f{u}", 16 * ACCS * (i + 1))
                    f = lambda a: a.rearrange("p t d -> p (t d)")
                    wait(e, f"v_o{u}", i)
                    e.tensor_tensor(f(fs[u][:, :, :]), f(fa[u][:, 2, :, :]), f(fa[u][:, 3, :, :]), ALU.add)
                    ch(e.tensor_tensor(f(fa[u][:, 0, :, :]), f(fa[u][:, 0, :, :]), f(fa[u][:, 1, :, :]), ALU.add))
                    e.tensor_tensor(f(fs[u][:, :, :]), f(fs[u][:, :, :]), f(fa[u][:, 0, :, :]), ALU.add)\
                        .then_inc(S_(f"v_f{u}"), 1)
                    wait(e, f"v_f{u}", i + 1)
                    for t in range(FT):
                        m = e.bn_stats(fst[u][:, t, :], fs[u][:, t, :])
                    ch(m, alone=True)
                    for t in range(FT):
                        m = e.bn_aggr(fag[u][:, t, :], fst[u][:, t, :])
                    ch(m)
                    ch(e.tensor_scalar(fve[u][:, :], fag[u][:, :, 1], LN_EPS, None, ALU.add))
                    e.tensor_copy(fmean[u][:, :], fag[u][:, :, 0]).then_inc(S_(f"v_fve{u}"), 1)
                    wait(e, f"g_f{u}", i + 1)
                    wait(e, f"st_out{u}", 16 * i)
                    for t in range(FT):
                        m = e.tensor_scalar(fo[u][:, t, :], fs[u][:, t, :], fmean[u][:, t:t + 1], frs[u][:, t:t + 1],
                                            ALU.subtract, ALU.mult)
                    m.then_inc(S_(f"v_o{u}"), 1)

        def pool_out(e):
            with e.Fori(0, N // (2 * FT * P)) as i:
                for u in range(2):
                    wait(e, f"v_fve{u}", i + 1)
                    e.tensor_tensor(frs[u][:, :], fve[u][:, :], fhalf[:, :], ALU.pow).then_inc(S_(f"g_f{u}"), 1)

        def act_out(e):
            with e.Fori(0, N // (2 * FT * P)) as i:
                for u in range(2):
                    wait(e, f"v_o{u}", i + 1)
                    e.dma_start(out[bass.ds((i * 2 + u) * FT * P, FT * P), :].rearrange("(t p) d -> p t d", p=P),
                                fo[u][:, :, :]).then_inc(S_(f"st_out{u}"), 16)
            for u in range(2):
                wait(e, f"st_out{u}", 16 * (N // (2 * FT * P)))

        @blk.tensor
        def _(e):
            pe_setup(e)

            def seq(i, more):
                pe_q(e, i)
                pe_kv(e, i)
                if more:
                    pe_z(e, i + 1)
                pe_scores2(e, i)
                if more:
                    pe_scores1(e, i + 1)
                pe_pT(e, i)
                if more:
                    pe_prT(e, i + 1)
                pe_av2(e, i)
                if more:
                    pe_av1(e, i + 1)
                pe_oT(e, i)
                pe_out2(e, i)
                if more:
                    pe_x1T(e, i + 1)
                pe_x2T(e, i)
                pe_router(e, i)
                pe_shared_in(e, i)
                pe_hsT(e, i)
                pe_shared_out(e, i)
                pe_rank(e, i)

            for step in (pe_z, pe_scores1, pe_prT, pe_av1, pe_x1T):
                step(e, 0)
            wait(e, "ld_w", 16 * 3)
            if nseq > 1:
                with e.Fori(0, nseq - 1) as i:
                    seq(i, True)
            seq(nseq - 1, False)
            pe_tables(e)
            wait(e, "ld_we", 16 * 4)

            first = experts(e, 0)
            pe_xbT(e, 0, 0)
            pe_xbT(e, 0, 1)
            pe_gu(e, 0, 0, first[0])
            pe_xbT(e, 0, 2)
            pe_gu(e, 0, 1, first[1])
            pe_hbT(e, 0, 0)
            with e.Fori(0, BLOCKS // UNROLL) as turn:
                b = turn
                w = experts(e, turn)
                for u in range(UNROLL):
                    pe_xbT(e, b, u + 3)
                    pe_gu(e, b, u + 2, w[u + 2])
                    pe_hbT(e, b, u + 1)
                    pe_down(e, b, u, w[u])

        def copy(e, o, i, done):
            e.activation(o, i, ACT.Copy).then_inc(S_(done), 1)

        def act_z(e, i):
            wait(e, "p_z", i + 1)
            wait(e, "p_s1", i)
            for k in range(DK):
                m = e.activation(zT[:, k, :], bank[0][:, k * S:(k + 1) * S], ACT.Identity, bias=g_bias[:, k, 0:1])
            m.then_inc(S_("a_z"), 1)
            wait(e, "p_vo", i + 1)
            copy(e, vo[:, :, :].rearrange("p t d -> p (t d)"), bank[1][:, :], "a_vo")

        def act_tanh(e, i):
            wait(e, "p_s1", i + 1)
            wait(e, "v_th", i)
            for t in range(T):
                e.activation(t1[:, t, :], bank[2][:, t * S:(t + 1) * S], ACT.Tanh, scale=0.5, bias=r_half[:, t:t + 1])
                m = e.activation(t2[:, t, :], bank[2][:, t * S:(t + 1) * S], ACT.Tanh, bias=r_sb[:, t:t + 1])
            m.then_inc(S_("a_tanh"), 1)

        def act_pr(e, i):
            wait(e, "v_mx", i + 1)
            wait(e, "p_prT", i)
            for t in range(T):
                m = e.activation(pr[:, t, :], th[:, t, :], ACT.Exp, scale=0.1, bias=nmx[:, t:t + 1],
                                 accum_out=den[:, t:t + 1])
            m.then_inc(S_("a_pr"), 1)

        def act_prT(e, i):
            wait(e, "p_prT", i + 1)
            wait(e, "p_av1", i)
            copy(e, prT[:, :, :, :].rearrange("p a b c -> p (a b c)"), bank[0][:, :], "a_prT")

        def act_q(e, i):
            wait(e, "p_q", i + 1)
            wait(e, "p_s2", i)
            for k in range(DK):
                m = e.activation(qT[:, k, :], bank[6][:, k * S:(k + 1) * S], ACT.Identity,
                                 bias=b_cross[:, k, 0:1])
            m.then_inc(S_("a_q"), 1)

        def act_sh(e, i):
            wait(e, "v_sh", i + 1)
            f = sh[:, :, :, :].rearrange("p a b c -> p (a b c)")
            e.activation(f, f, ACT.Exp, scale=HD ** -0.5).then_inc(S_("a_sh"), 1)

        def act_pT(e, i):
            for t in range(T):
                wait(e, "p_pT", 4 * i + 2 * t + 1)
                wait(e, "p_av2", 2 * i)
                copy(e, pT[:, t, 0:4, :].rearrange("p a b -> p (a b)"), bank[3 + 2 * t][:, :], "a_pT")

        def act_oT(e, i):
            wait(e, "p_oT", i + 1)
            wait(e, "p_out2", i)
            copy(e, oT[:, :, :].rearrange("p a b -> p (a b)"), bank[4][:, :], "a_oT")

        def act_x2T(e, i):
            wait(e, "p_x2T", i + 1)
            wait(e, "p_shin", i)
            copy(e, x2T[:, :, :].rearrange("p a b -> p (a b)"), bank[6][:, :], "a_x2T")

        def act_gates(e, i):
            wait(e, "p_router", i + 1)
            wait(e, "v_msel", i)
            e.activation(sc[:, :, :].rearrange("p a b -> p (a b)"), bank[7][:, 0:T * E], ACT.Tanh, scale=0.5)\
                .then_inc(S_("a_sc"), 1)
            wait(e, "p_shin", i + 1)
            wait(e, "v_hs", i)
            for t in range(T):
                m = e.activation(gt[:, t, :], bank[3 + t][:, 0:SH], ACT.Tanh, scale=0.5)
            m.then_inc(S_("a_hg"), 1)

        def act_hsT(e, i):
            wait(e, "p_hsT", i + 1)
            wait(e, "p_shout", i)
            copy(e, hsT[:, :, :].rearrange("p a b -> p (a b)"), bank[5][:, :], "a_hsT")

        def act_xbT(e, b, u):
            n = number(b, u)
            wait(e, "p_xbT", n + 1)
            wait(e, "p_gu", n - 1)
            copy(e, xbT[u % 2][:, :], bank[u % 2][:, 0:D], "a_xbT")

        def act_gb(e, b, u):
            n = number(b, u)
            wait(e, "p_gu", n + 1)
            wait(e, "v_hb", n - 1)
            e.activation(gb[u % 2][:, :], bank[2 + u % 2][:, 0:EI], ACT.Tanh, scale=0.5).then_inc(S_("a_gb"), 1)

        def act_yb(e, b, u):
            n = number(b, u)
            wait(e, "p_down", n + 1)
            wait(e, "v_wcol", n + 1)
            wait(e, f"st_acc{u % ACCS}", 16 * adds_before(b, u))
            e.activation(yb[u % ACCS][:, :], bank[6 + u % 2][:, 0:D], ACT.Copy, scale=wcol[u % 2][:, 0:1])\
                .then_inc(S_("a_yb"), 1)

        @blk.scalar
        def _(e):
            wait(e, "v_setup", 1)

            def seq(i, more):
                act_q(e, i)
                if more:
                    act_z(e, i + 1)
                act_sh(e, i)
                if more:
                    act_tanh(e, i + 1)
                act_pT(e, i)
                if more:
                    act_pr(e, i + 1)
                    act_prT(e, i + 1)
                act_oT(e, i)
                act_x2T(e, i)
                act_gates(e, i)
                act_hsT(e, i)

            for step in (act_z, act_tanh, act_pr, act_prT):
                step(e, 0)
            if nseq > 1:
                with e.Fori(0, nseq - 1) as i:
                    seq(i, True)
            seq(nseq - 1, False)
            wait(e, "v_tab", 1)
            act_xbT(e, 0, 0)
            act_xbT(e, 0, 1)
            act_gb(e, 0, 0)
            act_xbT(e, 0, 2)
            act_gb(e, 0, 1)
            with e.Fori(0, BLOCKS // UNROLL) as turn:
                b = turn
                for u in range(UNROLL):
                    act_xbT(e, b, u + 3)
                    act_gb(e, b, u + 2)
                    act_yb(e, b, u)
            act_out(e)

        NR = {"v1": 5, "v2": 30}

        def vec_r(e, i):
            ch = Chain(e, "v1", NR["v1"] * i)
            wait(e, "p_r", i + 1)
            wait(e, "a_tanh", i)
            ch(e.tensor_scalar(r_sb[:, :], bank[2][:, 0:T], c_bqbk[:, 0:1], None, ALU.add))
            e.tensor_scalar(r_half[:, :], r_sb[:, :], 0.5, None, ALU.mult)
            e.tensor_scalar(r_neg[:, :], r_sb[:, :], -1.0, None, ALU.mult).then_inc(S_("v_r"), 1)
            return ch

        def vec_th(e, i, ch):
            wait(e, "v_r", i + 1)
            wait(e, "a_tanh", i + 1)
            wait(e, "a_pr", i)
            for t in range(T):
                m = e.scalar_tensor_tensor(th[:, t, :], bank[2][:, t * S:(t + 1) * S], r_neg[:, t:t + 1],
                                           t1[:, t, :], ALU.max, ALU.add)
            ch(m)
            f = lambda a: a[:, :, :].rearrange("p a b -> p (a b)")
            e.scalar_tensor_tensor(f(th), f(t2), 1.5, f(th), ALU.mult, ALU.add).then_inc(S_("v_th"), 1)
            wait(e, "v_th", i + 1)
            ch(e.tensor_reduce(mx[:, :], th[:, :, :], AX.X, ALU.max))
            e.tensor_scalar(nmx[:, :], mx[:, :], -0.1, None, ALU.mult).then_inc(S_("v_mx"), 1)

        def layernorm(e, ch, stats, aggr, ve, told, wait_pow, i, src, rs, dst, done):
            for t in range(T):
                m = e.bn_stats(stats[:, t, :], src[:, t, :])
            ch(m, alone=True)
            for t in range(T):
                m = e.bn_aggr(aggr[:, t, :], stats[:, t, :])
            ch(m)
            e.tensor_scalar(ve[:, :], aggr[:, :, 1], LN_EPS, None, ALU.add).then_inc(S_(told), 1)
            wait(e, wait_pow, i + 1)
            for t in range(T):
                m = e.tensor_scalar(dst[:, t, 0:D], src[:, t, :], aggr[:, t, 0:1], rs[:, t:t + 1],
                                    ALU.subtract, ALU.mult)
            m.then_inc(S_(done), 1)

        def vec_x1(e, i, ch):
            wait(e, "p_av1", i + 1)
            wait(e, "a_pr", i + 1)
            wait(e, "g_xc", i + 1)
            e.reciprocal(den[:, :], den[:, :]).then_inc(S_("v_rd"), 1)
            wait(e, "v_rd", i + 1)
            for t in range(T):
                m = e.scalar_tensor_tensor(xc[:, t, :], bank[1][:, t * D:(t + 1) * D], den[:, t:t + 1],
                                           xc[:, t, :], ALU.mult, ALU.add)
            m.then_inc(S_("v_pre1"), 1)
            wait(e, "v_pre1", i + 1)
            wait(e, "p_x1T", i)
            wait(e, "g_xc2", i)
            layernorm(e, ch, st1, ag1, ve1, "v_ve1", "g_rs1", i, xc, rs1, x1, "v_x1")

        def vec_x1T(e, i):
            wait(e, "p_x1T", i + 1)
            wait(e, "p_q", i)
            e.tensor_copy(x1T[:, :, :].rearrange("p a b -> p (a b)"), bank[0][:, :]).then_inc(S_("v_x1T"), 1)

        def vec_kv(e, i):
            wait(e, "p_k", i + 1)
            wait(e, "p_s2", i)
            for k in range(DK):
                for hh in range(2):
                    m = e.tensor_scalar(kM[:, k, :, hh, :], bank[3][:, k * S:(k + 1) * S].rearrange(
                        "p (a b) -> p a b", b=CH), b_cross[:, k, 1:2], c("headmask")[:, hh:hh + 1], ALU.add, ALU.mult)
            m.then_inc(S_("v_k"), 1)
            wait(e, "p_v", i + 1)
            wait(e, "p_av2", 2 * i)
            mask = c("valmask")[:, 0:2 * HD].rearrange("p (a b) -> p a b", a=1).to_broadcast([P, NP, 2 * HD])
            for ch in range(S // CH):
                b, at = 4 + ch // 2, ch % 2 * D
                m = e.tensor_tensor(vM[:, ch, :, 0:2 * HD], bank[b][:, at:at + D].rearrange("p (a b) -> p a b", a=NP),
                                    mask, ALU.mult)
            m.then_inc(S_("v_v"), 1)

        def vec_sh(e, i):
            wait(e, "p_s2", i + 1)
            wait(e, "p_pT", 4 * i)
            for j in range(4):
                m = e.tensor_reduce(mxh[:, j, :, :, :].rearrange("p a b c -> p (a b c)"),
                                    bank[3 + j][:, :].rearrange("p (a b) -> p a b", b=CH), AX.X, ALU.max)
            m.then_inc(S_("v_mxh"), 1)
            wait(e, "v_mxh", i + 1)
            for j in range(4):
                most = mxh[:, j, :, :, :].rearrange("p a b (c o) -> p (a b c) o", o=1).to_broadcast([P, 8, CH])
                m = e.tensor_tensor(sh[:, j, :, :].rearrange("p a (b c) -> p (a b) c", c=CH),
                                    bank[3 + j][:, :].rearrange("p (a b) -> p a b", b=CH), most, ALU.subtract)
            m.then_inc(S_("v_sh"), 1)

        def vec_pT(e, i):
            for t in range(T):
                wait(e, "p_pT", 4 * i + 2 * t + 2)
                wait(e, "p_av2", 2 * i)
                e.tensor_copy(pT[:, t, 4:8, :].rearrange("p a b -> p (a b)"), bank[4 + 2 * t][:, :])\
                    .then_inc(S_("v_pT"), 1)

        def vec_o(e, i, ch):
            for t in range(T):
                wait(e, "p_av2", 2 * i + t + 1)
                if t == 0:
                    wait(e, "p_oT", i)
                av = bank[7 - 4 * t][:, 0:NP * VW].rearrange("p (a b) -> p a b", b=VW)
                ch(e.reciprocal(rden[:, t, :, :], av[:, :, 2 * HD:VW]))
                for hh in range(2):
                    m = e.tensor_tensor(
                        o_sb[:, t, :].rearrange("p (a h b) -> p a h b", h=2, b=HD)[:, :, hh, :],
                        av[:, :, hh * HD:(hh + 1) * HD],
                        rden[:, t, :, hh:hh + 1].to_broadcast([P, NP, HD]), ALU.mult)
            m.then_inc(S_("v_o"), 1)

        def vec_x2(e, i, ch):
            wait(e, "p_out2", i + 1)
            wait(e, "g_xc2", i + 1)
            f = lambda a: a[:, :, :].rearrange("p a b -> p (a b)")
            ch(e.tensor_tensor(f(xc2), bank[5][:, :], f(xc2), ALU.add))
            wait(e, "st_row", 16 * TOPK * T * i)
            layernorm(e, ch, st2, ag2, ve2, "v_ve2", "g_rs2", i, xc2, rs2, row, "v_x2")

        def vec_route(e, i, ch):
            wait(e, "a_sc", i + 1)
            ch(e.tensor_scalar(sc[:, :, :], sc[:, :, :], 0.5, 0.5, ALU.mult, ALU.add))
            rb = bias_router[:, :].rearrange("p (a b) -> p a b", a=1).to_broadcast([P, T, E])
            ch(e.tensor_tensor(sfc[:, :, :], sc[:, :, :], rb, ALU.add), alone=True)
            for t in range(T):
                for g in range(GRP):
                    m = e.max(g8[:, t, g, :], sfc[:, t, g * GE:(g + 1) * GE])
            ch(m)
            ch(e.tensor_tensor(gs[:, :, 0:GRP], g8[:, :, :, 0], g8[:, :, :, 1], ALU.add), alone=True)
            for t in range(T):
                m = e.max(gm[:, t, :], gs[:, t, :])
            ch(m)
            ch(e.tensor_copy(gv[:, :, 0:TOPG], gm[:, :, 0:TOPG]), alone=True)
            for t in range(T):
                m = e.match_replace(gr[:, t, :], gv[:, t, :], gs[:, t, :], BIG)
            ch(m)
            ch(e.tensor_scalar(gsel[:, :, :], gr[:, :, 0:GRP], BIG, None, ALU.is_ge))
            for t in range(T):
                m = e.tensor_tensor(tmp[:, t, 0:E].rearrange("p (a b) -> p a b", a=GRP),
                                    sfc[:, t, :].rearrange("p (a b) -> p a b", a=GRP),
                                    gsel[:, t, :].rearrange("p (a b) -> p a b", b=1).to_broadcast([P, GRP, GE]),
                                    ALU.mult)
            ch(m)
            ch(e.tensor_scalar(tmp[:, :, 0:E], tmp[:, :, 0:E], 0.0, None, ALU.add), alone=True)
            for t in range(T):
                m = e.max(em[:, t, :], tmp[:, t, 0:E])
            ch(m)
            ch(e.tensor_copy(ev[:, :, 0:TOPK], em[:, :, 0:TOPK]), alone=True)
            for t in range(T):
                m = e.match_replace(er[:, t, :], ev[:, t, :], tmp[:, t, :], BIG)
            ch(m)
            wait(e, "p_rank", i)
            ch(e.tensor_scalar(msel[:, :, :], er[:, :, 0:E], BIG, None, ALU.is_ge))
            ch(e.tensor_tensor(wraw[:, :, :], sc[:, :, :], msel[:, :, :], ALU.mult))
            ch(e.tensor_reduce(wsum[:, :], wraw[:, :, :], AX.X, ALU.add))
            ch(e.tensor_scalar(wsum[:, :], wsum[:, :], 1e-20, None, ALU.add))
            ch(e.reciprocal(wsum[:, :], wsum[:, :]))
            for t in range(T):
                m = e.tensor_scalar(row[:, t, D:D + E], wraw[:, t, :], wsum[:, t:t + 1], 0.5 * ROUTE_SCALE,
                                    ALU.mult, ALU.mult)
            ch(m)
            m = e.tensor_scalar(row[:, :, D + E].bitcast(I32), row[:, :, D + E].bitcast(I32), float(S), None, ALU.add)
            m.then_inc(S_("v_msel"), 1)

        def vec_hs(e, i, ch):
            wait(e, "a_hg", i + 1)
            wait(e, "p_hsT", i)
            for t in range(T):
                m = e.scalar_tensor_tensor(gt[:, t, :], gt[:, t, :], 1.0, bank[3 + t][:, 0:SH], ALU.add, ALU.mult)
            ch(m)
            for t in range(T):
                m = e.tensor_tensor(hs[:, t, :], gt[:, t, :], bank[3 + t][:, SH:2 * SH], ALU.mult)
            m.then_inc(S_("v_hs"), 1)

        def vec_key(e, i, ch):
            wait(e, "p_rank", i + 1)
            rank = bank[7][:, 128:128 + T * E].rearrange("p (a b) -> p a b", a=T)
            start = c("region").rearrange("p (a b) -> p a b", a=1).to_broadcast([P, T, E])
            ch(e.tensor_tensor(key[:, :, :], rank, start, ALU.add))
            for t in range(T):
                ch(e.tensor_tensor(macc[:, :], macc[:, :], msel[:, t, :], ALU.add))
            ch(e.tensor_tensor(key[:, :, :], key[:, :, :], msel[:, :, :], ALU.mult), alone=True)
            for t in range(T):
                m = e.max(slot[:, t, :], key[:, t, :])
            ch(m)
            wait(e, "st_row", 16 * TOPK * T * i)
            e.tensor_scalar(idx[:, :, :], slot[:, :, 0:TOPK], -1.0, None, ALU.add).then_inc(S_("v_key"), 1)

        def vec_acc(e, i):
            wait(e, "p_shout", i + 1)
            wait(e, "st_acc", 16 * i)
            for t in range(T):
                m = e.scalar_tensor_tensor(acc_sb[:, t, :], bank[6][:, t * D:(t + 1) * D], 0.5, row[:, t, 0:D],
                                           ALU.mult, ALU.add)
            m.then_inc(S_("v_acc"), 1)

        def vec_tables(e):
            ch = Chain(e, "vt", 0)
            wait(e, "p_tab", 1)
            ch(e.tensor_scalar(counts[:, :], bank[7][0:E, 0:1], float(P - 1), None, ALU.add))
            ch(e.tensor_tensor(padrow[:, :], bank[7][0:1, 32:32 + E], c("region", 1), ALU.add))
            ch(e.tensor_scalar(padrow[:, :], padrow[:, :], -1.0, None, ALU.add))
            ch(e.tensor_copy(cnt_i[:, :], counts[:, :]))
            ch(e.tensor_scalar(cnt_i[:, :], cnt_i[:, :], 7, None, ALU.logical_shift_right))
            e.tensor_copy(nblk[:, :], cnt_i[:, :]).then_inc(S_("v_nblk"), 1)
            wait(e, "p_tab", 2)
            ch(e.tensor_copy(upto[:, :], bank[7][0:E, 1:2]))
            e.tensor_scalar(past[:, :], c("blockno", E), upto[:, 0:1], None, ALU.is_ge).then_inc(S_("v_past"), 1)
            wait(e, "p_tab", 3)
            ch(e.tensor_tensor(tab[:, 0, :], c("blockno", 1), bank[6][0:1, TABLE:2 * TABLE], ALU.subtract))
            ch(e.tensor_scalar(tab[:, 0, :], tab[:, 0, :], float(P), None, ALU.mult))
            ch(e.tensor_scalar(tab[:, 1, :], bank[6][0:1, 0:TABLE], float(REGION), None, ALU.mult))
            ch(e.tensor_tensor(tab[:, 0, :], tab[:, 0, :], tab[:, 1, :], ALU.add))
            ch(e.tensor_scalar(tab_i[:, 0, :], tab[:, 0, :], float(E * REGION), None, ALU.min))
            ch(e.tensor_scalar(tab[:, 1, :], bank[6][0:1, 0:TABLE], float(E - 1), None, ALU.min))
            ch(e.tensor_copy(tab_i[:, 1, :], tab[:, 1, :]))
            for j in range(2):
                for v in reversed(range(WORD)):
                    at = j * WORD + v
                    x = tab_i[:, 1, at:at + BLOCKS - UNROLL + 1:UNROLL]
                    if v == WORD - 1:
                        ch(e.tensor_copy(words[:, :, j], x))
                    else:
                        ch(e.tensor_scalar(words[:, :, j], words[:, :, j], 5, None, ALU.logical_shift_left))
                        ch(e.tensor_tensor(words[:, :, j], words[:, :, j], x, ALU.bitwise_or))
            e.nop().then_inc(S_("v_tab"), 1)

        def vec_hb(e, b, u):
            n = number(b, u)
            wait(e, "a_gb", n + 1)
            e.scalar_tensor_tensor(hb1[u % 2][:, :], gb[u % 2][:, :], 1.0, bank[2 + u % 2][:, 0:EI],
                                   ALU.add, ALU.mult).then_inc(S_("v_hb1"), 1)
            wait(e, "v_hb1", n + 1)
            wait(e, "p_hbT", n - 1)
            e.tensor_tensor(hb[u % 2][:, :], hb1[u % 2][:, :], bank[2 + u % 2][:, EI:2 * EI], ALU.mult)\
                .then_inc(S_("v_hb"), 1)

        def vec_wcol(e, b, u, x):
            n = number(b, u)
            wait(e, f"ld_row{u % UNROLL}", 16 * loads_of_buffer(b, u))
            wait(e, "a_yb", n - 1)
            e.tensor_copy(wcol[u % 2][:, :], rowsb[u % UNROLL][:, bass.ds(x + D, 1)]).then_inc(S_("v_wcol"), 1)

        def vec_hbT(e, b, u):
            n = number(b, u)
            wait(e, "p_hbT", n + 1)
            wait(e, "p_down", n - 1)
            e.tensor_copy(hbT[u % 2][:, :], bank[4 + u % 2][:, 0:EI]).then_inc(S_("v_hbT"), 1)

        @blk.vector
        def _(e):
            ch = Chain(e, "vs", 0)
            e.memset(half_neg[:, :], -0.5).then_inc(S_("v_const"), 1)
            e.memset(fhalf[:, :], -0.5)
            e.memset(gs[:, :, :], -BIG)
            e.memset(gv[:, :, :], -BIG)
            e.memset(tmp[:, :, :], -BIG)
            e.memset(ev[:, :, :], -BIG)
            e.memset(pad[:, :], 0.0)
            ch(e.memset(macc[:, :], 0.0))
            wait(e, "g_iota", 2)
            e.tensor_copy(pad[:, D + E:RW].bitcast(I32), pad_id[:, :]).then_inc(S_("v_pad"), 1)
            ch(e.tensor_copy(row[:, :, D + E].bitcast(I32), tok_id[:, :]))
            wait(e, "ld_const", 16 * 7)
            for chk in range(S // CH):
                m = e.tensor_copy(vM[:, chk, :, 2 * HD:VW], c("valmask")[:, 2 * HD:VW].rearrange(
                    "p (a b) -> p a b", a=1).to_broadcast([P, NP, 2]))
            for k in range(DK):
                for j, b in enumerate((b_attn[:, k, 0:1], b_attn[:, k, 2:3], b_attn[:, k, 3:4])):
                    m = e.tensor_scalar(rep[:, k, j, :], c("ones"), b, None, ALU.mult)
            m.then_inc(S_("v_rep"), 1)
            wait(e, "p_setup", 1)
            e.tensor_copy(g_qk[:, :, :].rearrange("p a b -> p (a b)"), bank[0][:, :])
            e.tensor_copy(g_vo[:, :, :].rearrange("p a b -> p (a b)"), bank[1][:, :])
            e.tensor_copy(g_bias[:, :, :], bank[2][:, 0:4].rearrange("p (j k) -> p k j", j=2))
            e.tensor_copy(c_bqbk[:, :], bank[2][:, 8:9])
            e.tensor_copy(c_out[:, :, :].rearrange("p a b -> p (a b)"), bank[3][:, :]).then_inc(S_("v_setup"), 1)

            def one(i):
                ch1 = vec_r(e, i)
                vec_th(e, i, ch1)
                vec_x1(e, i, ch1)
                vec_x1T(e, i)

            def seq(i, more):
                ch2 = Chain(e, "v2", NR["v2"] * i)
                vec_kv(e, i)
                ch1 = vec_r(e, i + 1) if more else None
                vec_sh(e, i)
                if more:
                    vec_th(e, i + 1, ch1)
                vec_pT(e, i)
                vec_o(e, i, ch2)
                if more:
                    vec_x1(e, i + 1, ch1)
                vec_x2(e, i, ch2)
                if more:
                    vec_x1T(e, i + 1)
                    assert ch1.n == NR["v1"], ch1.n
                vec_route(e, i, ch2)
                vec_hs(e, i, ch2)
                vec_key(e, i, ch2)
                vec_acc(e, i)
                assert ch2.n == NR["v2"], ch2.n

            one(0)
            if nseq > 1:
                with e.Fori(0, nseq - 1) as i:
                    seq(i, True)
            seq(nseq - 1, False)
            vec_tables(e)

            wait(e, "v_tab", 1)

            vec_hb(e, 0, 0)
            vec_hb(e, 0, 1)
            vec_hbT(e, 0, 0)
            with e.Fori(0, BLOCKS // UNROLL) as turn:
                b = turn
                x = experts(e, turn)
                for u in range(UNROLL):
                    vec_hb(e, b, u + 2)
                    vec_hbT(e, b, u + 1)
                    vec_wcol(e, b, u, x[u])
            vec_out(e)

        def pool_xc(e, i):
            wait(e, "ld_x", 16 * (i + 1))
            wait(e, "v_x1", i)
            for t in range(T):
                m = e.tensor_tensor(xc[:, t, :], x_sb[:, t, :], c_out[:, 0, :], ALU.add)
            m.then_inc(S_("g_xc"), 1)

        def pool_rs(e, i, told, ve, rs, done):
            wait(e, told, i + 1)
            e.tensor_tensor(rs[:, :], ve[:, :], half_neg[:, :], ALU.pow).then_inc(S_(done), 1)

        def pool_xc2(e, i):
            wait(e, "v_x1", i + 1)
            wait(e, "v_x2", i)
            for t in range(T):
                m = e.tensor_tensor(xc2[:, t, :], x1[:, t, :], c_out[:, 1, :], ALU.add)
            m.then_inc(S_("g_xc2"), 1)

        def pool_scatter(e, i):
            wait_apart(e, ("v_key", i + 1),
                       ("v_msel", i + 1))
            for t in range(T):
                for k in range(TOPK):
                    e.indirect_dma_start(routed, bass.IndirectOffsetOnAxis(ap=idx[:, t, k:k + 1], axis=0),
                                         row[:, t, :], None).then_inc(S_("st_row"), 16)

        @blk.gpsimd
        def _(e):
            for name in LOOKED_BACK:
                e.nop().then_inc(S_(name), FIRST)
            e.iota(pad_id[:, :], [[0, 1]], base=N, channel_multiplier=1).then_inc(S_("g_iota"), 1)
            e.iota(tok_id[:, :], [[P, T]], base=-S, channel_multiplier=1).then_inc(S_("g_iota"), 1)
            wait(e, "v_pad", 1)
            for a in range(ACCS):
                e.dma_start(accs[a][N:N + P, :], pad[:, 0:D]).then_inc(S_(f"st_acc{a}"), 16)
            e.dma_start(routed[E * REGION:E * REGION + P, :], pad[:, :]).then_inc(S_("st_row"), 16)
            wait(e, "v_setup", 1)
            wait(e, "v_const", 1)
            pool_xc(e, 0)
            pool_rs(e, 0, "v_ve1", ve1, rs1, "g_rs1")
            pool_xc2(e, 0)

            def seq(i, more):
                if more:
                    pool_xc(e, i + 1)
                    pool_rs(e, i + 1, "v_ve1", ve1, rs1, "g_rs1")
                pool_rs(e, i, "v_ve2", ve2, rs2, "g_rs2")
                if more:
                    pool_xc2(e, i + 1)
                pool_scatter(e, i)

            if nseq > 1:
                with e.Fori(0, nseq - 1) as i:
                    seq(i, True)
            seq(nseq - 1, False)
            wait(e, "st_acc", 16 * nseq)
            wait(e, "st_zero", 16 * nseq * (ACCS - 1))
            with e.Fori(0, BLOCKS // UNROLL) as turn:
                b = turn
                for u in range(UNROLL):
                    n = number(b, u)
                    wait_apart(e, ("a_yb", n + 1),
                               (f"st_acc{u % ACCS}", 16 * adds_before(b, u)))
                    e.indirect_dma_start(
                        accs[u % ACCS], bass.IndirectOffsetOnAxis(ap=rowsb[u][:, D + E:RW].bitcast(I32), axis=0),
                        yb[u % ACCS][:, :], None, compute_op=ALU.add).then_inc(S_(f"st_acc{u % ACCS}"), 16)
            pool_out(e)

        @blk.sync
        def _(e):
            e.dma_start(const[:, :], d["const"]).then_inc(S_("ld_const"), 16)
            e.dma_start(w_attn[:, :, :, :], d["w_attn"]).then_inc(S_("ld_const"), 16)
            e.dma_start(b_attn[:, :, :], d["b_attn"]).then_inc(S_("ld_const"), 16)
            e.dma_start(b_cross[:, :, :], d["b_cross"]).then_inc(S_("ld_const"), 16)
            e.dma_start(bo_rows[:, :, :], d["bo_rows"]).then_inc(S_("ld_const"), 16)
            e.dma_start(w_cross[:, :, :, :], d["w_cross"]).then_inc(S_("ld_const"), 16)
            e.dma_start(bias_router[:, :], d["bias_router"]).then_inc(S_("ld_const"), 16)

            def load_x(i):
                wait_apart(e, ("p_vo", i), ("p_s1", i), ("p_r", i))
                e.dma_start(xT[:, :, :], d["xT"][bass.ds(i, 1), :, :].rearrange("a p (k s) -> p (a k) s", k=DK))\
                    .then_inc(S_("ld_xT"), 16)
                wait(e, "g_xc", i)
                e.dma_start(x_sb[:, :, :], d["x"][bass.ds(i, 1), :, :].rearrange("a (t p) d -> p (a t) d", p=P))\
                    .then_inc(S_("ld_x"), 16)

            def load_c(i):
                wait(e, "p_v", i)
                e.dma_start(cT[:, :, :, :, :].rearrange("p k c a s -> p (k c a s)"),
                            d["ctxT"][bass.ds(i, 1), :, :].rearrange("a p s -> p (a s)"))\
                    .then_inc(S_("ld_cT"), 16)

            def store_acc(i):
                wait(e, "v_acc", i + 1)
                e.dma_start(accs[0][bass.ds(i * S, S), :].rearrange("(t p) d -> p t d", p=P), acc_sb[:, :, :])\
                    .then_inc(S_("st_acc"), 16)

            load_x(0)
            load_c(0)
            e.dma_start(w_router[:, :, :], d["w_router"]).then_inc(S_("ld_w"), 16)
            e.dma_start(w_shared_in[:, :, :], d["w_shared_in"]).then_inc(S_("ld_w"), 16)
            e.dma_start(w_shared_out[:, :, :], d["w_shared_out"]).then_inc(S_("ld_w"), 16)
            wait(e, "v_pad", 1)
            with e.Fori(0, nseq) as i:
                for a in range(1, ACCS):
                    e.dma_start(accs[a][bass.ds(i * S, S), :].rearrange("(t p) d -> p t d", p=P),
                                pad[:, 0:D].rearrange("p (a d) -> p a d", a=1).to_broadcast([P, T, D]))\
                        .then_inc(S_("st_zero"), 16)
            PART = 8
            wait(e, "p_setup", 1)
            for g in range(E // PART):
                e.dma_start(w_expert[:, g * PART:(g + 1) * PART, :], d["w_expert"][:, g * PART:(g + 1) * PART, :])\
                    .then_inc(S_("ld_we"), 16)
            if nseq > 1:
                with e.Fori(0, nseq - 1) as i:
                    load_x(i + 1)
                    load_c(i + 1)
                    store_acc(i)
            store_acc(nseq - 1)
            wait(e, "v_tab", 1)
            with e.Fori(0, E) as x:
                at = e.value_load(padrow[0:1, bass.ds(x, 1)], min_val=0, max_val=E * REGION - P)
                e.dma_start(routed[bass.ds(at, P), :], pad[:, :]).then_inc(S_("st_pad"), 16)
            wait(e, "st_row", 16 * TOPK * T * nseq)
            wait(e, "st_acc", 16 * nseq)
            wait(e, "st_pad", 16 * E)

            def load_rows(turn, u):
                at = e.value_load(tab_i[0:1, 0, bass.ds(number(turn, u), 1)], min_val=0, max_val=E * REGION)
                if not isinstance(turn, int):
                    wait_apart(e, ("p_xbT", number(turn, u) - UNROLL + 1),
                               ("v_wcol", number(turn, u) - UNROLL + 1))
                    wait_apart(e, (f"st_acc{u % ACCS}", 16 * (adds_before(turn, u) - UNROLL // ACCS + 1)))
                e.dma_start(rowsb[u][:, :], routed[bass.ds(at, P), :]).then_inc(S_(f"ld_row{u}"), 16)

            for u in range(UNROLL):
                load_rows(0, u)
            with e.Fori(1, TABLE // UNROLL) as turn:
                for u in range(UNROLL):
                    load_rows(turn, u)
            sync_out(e)



_SHARED = ("w_attn", "b_attn", "b_cross", "bo_rows", "w_cross", "bias_router", "w_router", "w_shared_in",
           "w_shared_out", "w_expert")


def layouts(i):
    f = lambda n: np.asarray(i[n])
    rows = lambda w: w.reshape(DK, P, *w.shape[1:]).swapaxes(0, 1)
    x, ctx = f("x"), f("ctx_1024")
    cols = lambda a: a.transpose(0, 2, 1).reshape(-1, DK, P, S).transpose(0, 2, 1, 3).reshape(-1, P, DK * S)
    ip, ib = f("L0_xattn_in_proj_w"), f("L0_xattn_in_proj_b")
    gu = np.concatenate([f("L0_ffn_gate_w"), f("L0_ffn_up_w")], axis=1)
    gu = gu.transpose(2, 0, 1).reshape(DK, P, E, 2 * EI).transpose(1, 2, 0, 3).reshape(P, E, 2 * D)
    return {
        "x": x,
        "xT": cols(x),
        "ctxT": np.repeat(cols(ctx).reshape(-1, P, DK * S // CH, 1, CH), 2, axis=3).reshape(-1, P, 2 * DK * S),
        "w_attn": np.stack([rows(f("L0_attn_Wq")), rows(f("L0_attn_Wk")), rows(f("L0_attn_Wv")),
                            rows(f("L0_attn_Wo").T)], axis=2),
        "b_attn": np.stack([rows(f("L0_attn_bq")), rows(f("L0_attn_bk")), rows(f("L0_attn_bv")),
                            rows(ib[2 * D:])], axis=2),
        "b_cross": np.stack([rows(ib[:D]), rows(ib[D:2 * D])], axis=2),
        "bo_rows": np.stack([f("L0_attn_bo"), f("L0_xattn_out_proj_b")])[None],
        "w_cross": np.stack([rows(ip[:D].T), rows(ip[D:2 * D].T), rows(ip[2 * D:].T),
                             rows(f("L0_xattn_out_proj_w").T)], axis=2),
        "bias_router": np.tile(f("L0_ffn_router_bias"), (P, 1)),
        "w_router": rows(f("L0_ffn_router_weight").T),
        "w_shared_in": rows(np.concatenate([f("L0_ffn_shared_gate_w"), f("L0_ffn_shared_up_w")], axis=0).T),
        "w_shared_out": rows(f("L0_ffn_shared_down_w").T),
        "w_expert": np.concatenate([gu, f("L0_ffn_down_w").transpose(2, 0, 1)], axis=2),
        "const": constants(x.shape[0])[1],
    }


def kernel(**inputs):
    import concourse.bacc as bacc
    from concourse.bass_utils import run_bass_kernel_spmd

    nc = bacc.Bacc("TRN2", target_bir_lowering=False, num_devices=1)
    arrays = {name: np.ascontiguousarray(a) for name, a in layouts(inputs).items()}
    d = {name: nc.dram_tensor(name, a.shape, mybir.dt.from_np(a.dtype), kind="ExternalInput").ap()
         for name, a in arrays.items()}
    shape = arrays["x"].shape
    out = nc.dram_tensor("out", (shape[0] * S, D), mybir.dt.float32, kind="ExternalOutput").ap()
    build(nc, d, out)
    r = run_bass_kernel_spmd(nc, [arrays], core_ids=[0])
    return r.results[0]["out"].reshape(shape)
```

```python
import numpy as np
import concourse.bass as bass
from concourse import mybir
from contextlib import ExitStack

P = 128
D = 256
DK = D // P
S = 256
T = S // P
H, HD = 16, 16
CH = 64
NP = H // 2
E, EI = 32, 128
GRP, GE = 4, E // 4
TOPK, TOPG = 4, 2
SH = 256
ROUTE_SCALE = 2.5
LN_EPS = 1e-5
BIG = 1e30

RW = D + E + 1
ACCS = 4
UNROLL = 8
FT = 2
STEPS = 4
WORD = 6
VW = 2 * (2 * HD + 2)


def shapes(nseq):
    n = nseq * S
    blocks = n * TOPK // P + E
    blocks = -(-blocks // UNROLL) * UNROLL
    return n, n + P, blocks


def constants(nseq):
    n, region, blocks = shapes(nseq)
    p = np.arange(P)
    table = blocks + UNROLL
    parts = [
        np.eye(P),
        (p[:, None] < p[None, :]),
        np.ones((P, P)),
        (p[:, None] // HD % 2 == np.arange(2)[None]),
        (p[:, None] // CH == np.arange(2)[None]),
        np.tile(np.arange(E) * region + 1.0, (P, 1)),
        (p[:, None] <= np.arange(E)[None]),
        np.tile(np.arange(table), (P, 1)),
    ]
    at, out = 0, {}
    for name, a in zip(("ident", "before", "ones", "headmask", "valmask", "region", "upto", "blockno"), parts):
        out[name] = (at, a.shape[1])
        at += a.shape[1]
    return out, np.concatenate([a.astype(np.float32) for a in parts], axis=1)


def build(nc, d, out):
    F32, I32 = mybir.dt.float32, mybir.dt.int32
    ALU, ACT, AX = mybir.AluOpType, mybir.ActivationFunctionType, mybir.AxisListType
    nseq = d["x"].shape[0]
    N, REGION, BLOCKS = shapes(nseq)
    CC, _ = constants(nseq)
    TABLE = BLOCKS + UNROLL

    routed = nc.dram_tensor("routed", ((E + 1) * REGION, RW), F32).ap()
    accs = [nc.dram_tensor(f"acc{a}", (N + P, D), F32).ap() for a in range(ACCS)]

    ctx = ExitStack()
    with ctx:
        def sb(name, shape, dt=F32):
            return ctx.enter_context(nc.sbuf_tensor(f"{name}_tile", shape, dt))

        def sem(name):
            return ctx.enter_context(nc.semaphore(name))

        bank = [ctx.enter_context(nc.psum_tensor(f"bank{b}", [P, 512], F32)) for b in range(8)]

        const = sb("const", [P, sum(w for _, w in CC.values())])

        def c(name, rows=P):
            at, w = CC[name]
            return const[0:rows, at:at + w]

        ident = c("ident")
        w_attn = sb("w_attn", [P, DK, 4, D])
        b_attn = sb("b_attn", [P, DK, 4])
        b_cross = sb("b_cross", [P, DK, 2])
        bo_rows = sb("bo_rows", [1, 2, D])
        w_cross = sb("w_cross", [P, DK, 4, D])
        w_router = sb("w_router", [P, DK, E])
        bias_router = sb("bias_router", [P, E])
        w_shared_in = sb("w_shared_in", [P, DK, 2 * SH])
        w_shared_out = sb("w_shared_out", [P, DK, D])
        w_expert = sb("w_expert", [P, E, 3 * D])
        w_flat = w_expert[:, :, :].rearrange("p e n -> p (e n)")
        rep = w_flat[:, 0:DK * 3 * P].rearrange("p (k j n) -> p k j n", k=DK, j=3)
        g_qk = sb("g_qk", [P, DK, D])
        g_vo = sb("g_vo", [P, DK, D])
        g_bias = sb("g_bias", [P, DK, 2])
        bk_masked = sb("bk_masked", [P, DK, 2])
        c_bqbk = sb("c_bqbk", [P, 1])
        c_out = sb("c_out", [P, 2, D])

        pad = sb("pad", [P, RW])
        counts = sb("counts", [E, 1])
        cnt_i = sb("cnt_i", [E, 1], I32)
        nblk = sb("nblk", [E, 1])
        upto = sb("upto", [E, 1])
        padrow = sb("padrow", [1, E], I32)
        fhalf = sb("fhalf", [P, FT])
        pad_id = sb("pad_id", [P, 1], I32)
        tok_id = sb("tok_id", [P, T], I32)
        macc = sb("macc", [P, T, E])

        ctx_a = ExitStack()

        def sa(name, shape, dt=F32):
            return ctx_a.enter_context(nc.sbuf_tensor(f"{name}_tile", shape, dt))

        x_sb = sa("x_sb", [P, T, D])
        xT = sa("xT", [P, DK, S])
        cT = sa("cT", [P, DK, T, 3, CH])
        zT = sa("zT", [P, DK, S])
        vo = sa("vo", [P, T, D])
        r_sb = sa("r_sb", [P, T])
        r_half = sa("r_half", [P, T])
        r_neg = sa("r_neg", [P, T])
        t1 = sa("t1", [P, T, S])
        t2 = sa("t2", [P, T, S])
        th = sa("th", [P, T, S])
        mx = sa("mx", [P, T])
        nmx = sa("nmx", [P, T])
        pr = sa("pr", [P, T, S])
        den = sa("den", [P, T])
        prT = sa("prT", [P, T, T, P])
        xc = sa("xc", [P, T, D])
        st1 = sa("st1", [P, T, 6])
        ag1 = sa("ag1", [P, T, 2])
        ve1 = sa("ve1", [P, T])
        rs1 = sa("rs1", [P, T])
        x1 = sa("x1", [P, T, D])
        x1T = sa("x1T", [P, DK, S])
        half_neg = sa("half_neg", [P, T])
        qT = sa("qT", [P, DK, S])
        kM = sa("kM", [P, DK, S // CH, 2, CH])
        vM = sa("vM", [P, T, NP, VW])
        mxh = sa("mxh", [P, 4, T, 2, 2])
        sh = sa("sh", [P, 4, T, 4 * CH])
        pT = sa("pT", [P, T, NP, P])
        rden = sa("rden", [P, T, NP, 4])
        o_sb = sa("o_sb", [P, T, D])
        oT = sa("oT", [P, DK, S])
        xc2 = sa("xc2", [P, T, D])
        st2 = sa("st2", [P, T, 6])
        ag2 = sa("ag2", [P, T, 2])
        ve2 = sa("ve2", [P, T])
        rs2 = sa("rs2", [P, T])
        row = sa("row", [P, T, RW])
        x2 = sa("x2", [P, T, D])
        x2T = sa("x2T", [P, DK, S])
        hs = sa("hs", [P, T, SH])
        hsT = sa("hsT", [P, DK, S])
        acc_sb = sa("acc_sb", [P, T, D])
        sc = sa("sc", [P, T, E])
        sfc = sa("sfc", [P, T, E])
        g8 = sa("g8", [P, T, GRP, 8])
        gs = sa("gs", [P, T, GRP + 6])
        gm = sa("gm", [P, T, 8])
        gv = sa("gv", [P, T, 8])
        gr = sa("gr", [P, T, GRP + 6])
        gsel = sa("gsel", [P, T, GRP])
        tmp = sa("tmp", [P, T, E + 4])
        em = sa("em", [P, T, 8])
        ev = sa("ev", [P, T, 8])
        er = sa("er", [P, T, E + 4])
        msel = sa("msel", [P, T, E])
        wsum = sa("wsum", [P, T])
        wraw = sa("wraw", [P, T, E])
        key = sa("key", [P, T, E])
        slot = sa("slot", [P, T, 8])
        idx = sa("idx", [P, T, TOPK], I32)

        ctx_a.close()

        past = sb("past", [E, TABLE])
        tab = sb("tab", [1, 2, TABLE])
        tab_i = sb("tab_i", [1, 2, TABLE], I32)
        words = sb("words", [1, BLOCKS // UNROLL, 2], I32)
        rowsb = [sb(f"rowsb{u}", [P, RW]) for u in range(UNROLL)]
        xbT = [sb(f"xbT{u}", [P, D]) for u in range(2)]
        wcol = [sb(f"wcol{u}", [P, 1]) for u in range(UNROLL)]
        idcol = [sb(f"idcol{u}", [P, 1], I32) for u in range(UNROLL)]
        gb = [sb(f"gb{u}", [P, EI]) for u in range(2)]
        hb1 = [sb(f"hb1_{u}", [P, EI]) for u in range(2)]
        hb = [sb(f"hb{u}", [P, EI]) for u in range(2)]
        hbT = [sb(f"hbT{u}", [P, EI]) for u in range(2)]
        yb = [sb(f"yb{u}", [P, D]) for u in range(ACCS)]

        fa = [sb(f"fa{u}", [P, ACCS, FT, D]) for u in range(STEPS)]
        fs = [sb(f"fs{u}", [P, FT, D]) for u in range(STEPS)]
        fo = [sb(f"fo{u}", [P, FT, D]) for u in range(STEPS)]
        fst = [sb(f"fst{u}", [P, FT, 6]) for u in range(STEPS)]
        fag = [sb(f"fag{u}", [P, FT, 2]) for u in range(STEPS)]
        fmean = [sb(f"fmean{u}", [P, FT]) for u in range(STEPS)]
        fve = [sb(f"fve{u}", [P, FT]) for u in range(STEPS)]
        frs = [sb(f"frs{u}", [P, FT]) for u in range(STEPS)]

        names = {}

        def S_(name):
            if name not in names:
                names[name] = sem(name)
            return names[name]

        class Chain:

            def __init__(self, eng, name, base):
                self.eng, self.name, self.sem, self.base, self.n = eng, name, S_(name), base, 0

            def __call__(self, ins, alone=False):
                self.n += 1
                ins.then_inc(self.sem, 1)
                if alone:
                    wait_apart(self.eng, (self.name, self.base + self.n))
                else:
                    self.eng.wait_ge(self.sem, self.base + self.n)

        FIRST = UNROLL
        LOOKED_BACK = (
            "v_x1T", "v_pre1", "v_th", "a_tanh", "v_hs", "a_hsT", "v_acc", "v_key", "p_s1", "p_prT", "p_av1", "p_s2",
            "p_av2", "p_out2", "p_shin", "v_msel", "p_shout", "a_pr", "p_x1T", "g_xc2", "p_q", "p_pT", "p_oT",
            "p_rank", "p_hsT", "p_x2T", "g_row", "v_o", "a_oT", "v_pre2", "v_x1", "v_x2", "st_acc",
            "a_xbT", "v_hb", "a_yb", "p_gu", "p_hbT", "p_down",
            *(f"{n}{u}" for n in ("v_f", "v_o", "st_out") for u in range(STEPS)))
        STARTED = ("st_row", *(f"st_acc{a}" for a in range(ACCS)))

        def wait(e, name, value):
            if not isinstance(value, int) or value > 0:
                e.wait_ge(S_(name), value + (FIRST if name in LOOKED_BACK else 16 if name in STARTED else 0))

        def wait_apart(e, *waits):
            for name, value in waits:
                wait(e, name, value)
                e.nop().then_inc(S_("apart"), 1)

        def number(turn, u):
            return turn * UNROLL + u

        def loads_of_buffer(turn, u):
            return turn + (u // UNROLL + 1)

        def adds_before(turn, u):
            return turn * (UNROLL // ACCS) + u // ACCS

        def pad_rows(e, first, last):
            wait(e, "v_padrow", 1)
            with e.Fori(first, last) as x:
                at = e.value_load(padrow[0:1, bass.ds(x, 1)], min_val=0, max_val=E * REGION - P)
                e.dma_start(routed[bass.ds(at, P), :], pad[:, :]).then_inc(S_("st_pad"), 16)

        def experts(e, turn):
            out = []
            for j in range(2):
                w = e.value_load(words[0:1, bass.ds(turn, 1), j], min_val=0, max_val=E ** WORD - 1)
                out += [w // E ** v % E for v in range(WORD)]
            return out

        blk = ctx.enter_context(nc.Block())

        PARTS = 4
        SELF, CROSS, MIX, PLACE = range(PARTS)

        def run_stage_a(e, steps, before=lambda seqs: None, after=lambda args: None):
            def turn(seqs):
                args = before(seqs)
                for part, step in steps:
                    if seqs[part] is not None:
                        step(e, seqs[part], *(() if args is None else (args[part],)))
                after(args)

            def filled(t):
                return [t - part if 0 <= t - part < nseq else None for part in range(PARTS)]

            full = range(PARTS - 1, nseq)
            for t in range(min(PARTS - 1, nseq)):
                turn(filled(t))
            if len(full) > 0:
                with e.Fori(0, len(full)) as i:
                    turn([i + (PARTS - 1 - part) for part in range(PARTS)])
            for t in range(nseq, nseq + PARTS - 1):
                turn(filled(t))

        def transpose(e, o, i):
            return e.transpose(o, i, ident)

        def pe_setup(e):
            wait(e, "ld_const", 16 * 7)
            for db in range(DK):
                for k in range(DK):
                    e.matmul(bank[0][:, db * D:(db + 1) * D], w_attn[:, k, 0, db * P:(db + 1) * P],
                             w_attn[:, k, 1, :], start=k == 0, stop=k == DK - 1)
            for db in range(DK):
                for k in range(DK):
                    e.matmul(bank[1][:, db * D:(db + 1) * D], w_attn[:, k, 2, db * P:(db + 1) * P],
                             w_attn[:, k, 3, :], start=k == 0, stop=k == DK - 1)
            for j in range(2):
                for db in range(DK):
                    for k in range(DK):
                        e.matmul(bank[2][:, 2 * j + db:2 * j + db + 1], w_attn[:, k, 1 - j, db * P:(db + 1) * P],
                                 b_attn[:, k, j:j + 1], start=k == 0, stop=k == DK - 1)
            wait(e, "v_rep", 1)
            for k in range(DK):
                e.matmul(bank[2][:, 8:9], rep[:, k, 0, :], b_attn[:, k, 1:2], start=k == 0, stop=k == DK - 1)
            for j, (w, wi) in enumerate(((w_attn, 3), (w_cross, 3))):
                for k in range(DK):
                    e.matmul(bank[3][:, j * D:(j + 1) * D], rep[:, k, 1 + j, :], w[:, k, wi, :],
                             start=k == 0, stop=False)
                m = e.matmul(bank[3][:, j * D:(j + 1) * D], c("ones", 1), bo_rows[:, j, :], start=False, stop=True)
            m.then_inc(S_("p_setup"), 1)
            wait(e, "v_setup", 1)

        def pe_z(e, i):
            wait(e, "ld_xT", 16 * (i + 1))
            wait(e, "v_x1T", i)
            for db in range(DK):
                for k in range(DK):
                    m = e.matmul(bank[0][:, db * S:(db + 1) * S], g_qk[:, k, db * P:(db + 1) * P], xT[:, k, :],
                                 start=k == 0, stop=k == DK - 1)
            m.then_inc(S_("p_z"), 1)
            wait(e, "v_pre1", i)
            for t in range(T):
                for k in range(DK):
                    m = e.matmul(bank[1][:, t:t + 1], xT[:, k, t * P:(t + 1) * P], g_bias[:, k, 1:2],
                                 start=k == 0, stop=k == DK - 1)
            m.then_inc(S_("p_r"), 1)

        def pe_vo(e, i):
            wait(e, "a_z", i + 1)
            for t in range(T):
                for k in range(DK):
                    m = e.matmul(bank[0][:, t * D:(t + 1) * D], xT[:, k, t * P:(t + 1) * P], g_vo[:, k, :],
                                 start=k == 0, stop=k == DK - 1)
            m.then_inc(S_("p_vo"), 1)

        def pe_scores1(e, i):
            wait(e, "a_z", i + 1)
            wait(e, "v_r", i + 1)
            for t in range(T):
                for k in range(DK):
                    m = e.matmul(bank[1][:, t * S:(t + 1) * S], zT[:, k, t * P:(t + 1) * P], xT[:, k, :],
                                 start=k == 0, stop=k == DK - 1)
            m.then_inc(S_("p_s1"), 1)

        def pe_prT(e, i):
            wait(e, "a_pr", i + 1)
            wait(e, "a_vo", i + 1)
            for t in range(T):
                for u in range(T):
                    m = transpose(e, bank[0][:, (t * T + u) * P:(t * T + u + 1) * P], pr[:, t, u * P:(u + 1) * P])
            m.then_inc(S_("p_prT"), 1)

        def pe_av1(e, i):
            wait(e, "a_prT", i + 1)
            for t in range(T):
                for u in range(T):
                    m = e.matmul(bank[1][:, t * D:(t + 1) * D], prT[:, t, u, :], vo[:, u, :],
                                 start=u == 0, stop=u == T - 1)
            m.then_inc(S_("p_av1"), 1)

        def pe_x1T(e, i):
            wait(e, "v_x1", i + 1)
            for k in range(DK):
                for t in range(T):
                    m = transpose(e, bank[0][:, k * S + t * P:k * S + (t + 1) * P], x1[:, t, k * P:(k + 1) * P])
            m.then_inc(S_("p_x1T"), 1)

        def pe_kv(e, i):
            wait(e, "ld_cT", 16 * (i + 1))
            wait(e, "v_o", i)
            for db in range(DK):
                for k in range(DK):
                    m = e.matmul(bank[2][:, db * S:(db + 1) * S], w_cross[:, k, 1, db * P:(db + 1) * P],
                                 cT[:, k, :, 0:2, :],
                                 start=k == 0, stop=k == DK - 1)
            m.then_inc(S_("p_k"), 1)
            wait(e, "a_oT", i)
            for t in range(T):
                for h in range(2):
                    for k in range(DK):
                        m = e.matmul(bank[3 + t][:, h * P:(h + 1) * P],
                                     cT[:, k, t, h:h + 2, :].rearrange("p a c -> p (a c)"),
                                     w_cross[:, k, 2, :].rearrange("p (n h d) -> p n h d", h=2, d=HD)[:, :, h, :],
                                     start=k == 0, stop=k == DK - 1)
            m.then_inc(S_("p_v"), 1)

        def pe_q(e, i):
            wait(e, "v_x1T", i + 1)
            wait(e, "v_pre2", i)
            for db in range(DK):
                for k in range(DK):
                    m = e.matmul(bank[5][:, db * S:(db + 1) * S], w_cross[:, k, 0, db * P:(db + 1) * P], x1T[:, k, :],
                                 start=k == 0, stop=k == DK - 1)
            m.then_inc(S_("p_q"), 1)

        def pe_scores2(e, i):
            wait(e, "a_q", i + 1)
            wait(e, "a_k", i + 1)
            wait(e, "a_v", i + 1)
            for t in range(T):
                for hf in range(DK):
                    for a in range(2):
                        for j in range(4):
                            ch, rows = 2 * t + a, slice(32 * j, 32 * j + 32)
                            at = (t * DK + hf) * 2 * CH
                            m = e.matmul(bank[2 + j][a * CH:(a + 1) * CH, at:at + 2 * CH],
                                         qT[rows, hf, ch * CH:(ch + 1) * CH],
                                         kM[rows, hf, ch, :, :], start=True, stop=True)
            m.then_inc(S_("p_s2"), 1)

        def pe_pT(e, i):
            wait(e, "v_sh", T * (i + 1))
            for t in range(T):
                wait(e, "a_sh", T * i + t + 1)
                for hf in range(DK):
                    for j in range(4):
                        m = transpose(e, bank[2 + 2 * t + hf][:, j * P:(j + 1) * P], sh[:, j, t, hf * P:(hf + 1) * P])
                    m.then_inc(S_("p_pT"), 1)

        def pe_av2(e, i):
            for t in range(T):
                wait(e, "a_pT", 2 * i + t + 1)
                wait(e, "v_pT", 2 * i + t + 1)
                for j in range(NP):
                    at = j % 4 * VW
                    m = e.matmul(bank[2 + 2 * t + j // 4][:, at:at + VW], pT[:, t, j, :], vM[:, t, j, :],
                                 start=True, stop=True)
                m.then_inc(S_("p_av2"), 1)

        def pe_oT(e, i):
            wait(e, "v_o", i + 1)
            for k in range(DK):
                for t in range(T):
                    m = transpose(e, bank[3][:, k * S + t * P:k * S + (t + 1) * P], o_sb[:, t, k * P:(k + 1) * P])
            m.then_inc(S_("p_oT"), 1)

        def pe_out2(e, i):
            wait(e, "a_oT", i + 1)
            for t in range(T):
                for k in range(DK):
                    m = e.matmul(bank[5][:, t * D:(t + 1) * D], oT[:, k, t * P:(t + 1) * P], w_cross[:, k, 3, :],
                                 start=k == 0, stop=k == DK - 1)
            m.then_inc(S_("p_out2"), 1)

        def pe_x2T(e, i):
            wait(e, "v_x2", i + 1)
            wait(e, "v_key", i)
            for k in range(DK):
                for t in range(T):
                    m = transpose(e, bank[6][:, k * S + t * P:k * S + (t + 1) * P], x2[:, t, k * P:(k + 1) * P])
            m.then_inc(S_("p_x2T"), 1)

        def pe_router(e, i):
            wait(e, "a_x2T", i + 1)
            wait(e, "v_acc", i)
            wait(e, "ld_w", 16 * 3)
            for t in range(T):
                for k in range(DK):
                    m = e.matmul(bank[7][:, t * E:(t + 1) * E], x2T[:, k, t * P:(t + 1) * P], w_router[:, k, :],
                                 start=k == 0, stop=k == DK - 1)
            m.then_inc(S_("p_router"), 1)

        def pe_shared_in(e, i):
            for t in range(T):
                if t == 1:
                    wait(e, "a_sc", i + 1)
                for k in range(DK):
                    m = e.matmul(bank[6 + t][:, :], x2T[:, k, t * P:(t + 1) * P], w_shared_in[:, k, :],
                                 start=k == 0, stop=k == DK - 1)
                m.then_inc(S_("p_shin"), 1)

        def pe_hsT(e, i):
            wait(e, "v_hs", i + 1)
            for k in range(DK):
                for t in range(T):
                    m = transpose(e, bank[6][:, k * S + t * P:k * S + (t + 1) * P], hs[:, t, k * P:(k + 1) * P])
            m.then_inc(S_("p_hsT"), 1)

        def pe_shared_out(e, i):
            wait(e, "a_hsT", i + 1)
            for t in range(T):
                for k in range(DK):
                    m = e.matmul(bank[7][:, t * D:(t + 1) * D], hsT[:, k, t * P:(t + 1) * P], w_shared_out[:, k, :],
                                 start=k == 0, stop=k == DK - 1)
            m.then_inc(S_("p_shout"), 1)

        def pe_rank(e, i):
            wait(e, "v_msel", i + 1)
            f = lambda a: a[:, :, :].rearrange("p t x -> p (t x)")
            e.matmul(bank[6][:, 0:T * E], c("before"), f(msel), start=True, stop=False)
            m = e.matmul(bank[6][:, 0:T * E], c("ones"), f(macc), start=False, stop=True)
            m.then_inc(S_("p_rank"), 1)

        def pe_tables(e):
            wait(e, "v_key", nseq)
            wait(e, "v_acc", nseq)
            e.matmul(bank[7][0:E, 0:1], macc[:, 0, :], c("ones")[:, 0:1], start=True, stop=True)
            e.matmul(bank[7][0:1, 32:32 + E], c("ones")[:, 0:1], macc[:, 0, :], start=True, stop=True)\
                .then_inc(S_("p_tab"), 1)
            wait(e, "v_nblk", 1)
            e.matmul(bank[7][0:E, 1:2], c("upto", E), nblk[:, :], start=True, stop=True).then_inc(S_("p_tab"), 1)
            wait(e, "v_past", 1)
            e.matmul(bank[6][0:1, 0:TABLE], c("ones", E)[:, 0:1], past[:, :], start=True, stop=True)
            e.matmul(bank[6][0:1, TABLE:2 * TABLE], nblk[:, :], past[:, :], start=True, stop=True)\
                .then_inc(S_("p_tab"), 1)
            wait(e, "v_tab", 1)

        def pe_xbT(e, b, u):
            wait(e, f"ld_row{u % UNROLL}", 16 * loads_of_buffer(b, u))
            n = number(b, u)
            wait(e, "a_xbT", n - 1)
            for k in range(DK):
                m = transpose(e, bank[u % 2][:, k * P:(k + 1) * P], rowsb[u % UNROLL][:, k * P:(k + 1) * P])
            m.then_inc(S_("p_xbT"), 1)

        def pe_gu(e, b, u, w):
            n = number(b, u)
            wait(e, "a_xbT", n + 1)
            wait(e, "v_hb", n - 1)
            for k in range(DK):
                m = e.matmul(bank[2 + u % 2][:, 0:2 * EI], xbT[u % 2][:, k * P:(k + 1) * P],
                             w_flat[:, bass.ds(w * 3 * D + k * D, D)], start=k == 0, stop=k == DK - 1)
            m.then_inc(S_("p_gu"), 1)

        def pe_hbT(e, b, u):
            n = number(b, u)
            wait(e, "v_hb", n + 1)
            transpose(e, bank[4 + u % 2][:, 0:P], hb[u % 2][:, :]).then_inc(S_("p_hbT"), 1)

        def pe_down(e, b, u, w):
            n = number(b, u)
            wait(e, "v_hbT", n + 1)
            wait(e, "a_yb", n - 1)
            e.matmul(bank[6 + u % 2][:, 0:D], hbT[u % 2][:, :], w_flat[:, bass.ds(w * 3 * D + 2 * D, D)],
                     start=True, stop=True).then_inc(S_("p_down"), 1)

        TURNS = N // (STEPS * FT * P)

        def rows_of(turn, u):
            return bass.ds((turn * STEPS + u) * FT * P, FT * P)

        def flat(a):
            return a.rearrange("p t d -> p (t d)")

        def staggered(first, second):
            for u in range(STEPS + 1):
                if u < STEPS:
                    first(u)
                if u > 0:
                    second(u - 1)

        def sync_out(e):
            for a in range(ACCS):
                wait(e, f"st_acc{a}", 16 * BLOCKS // ACCS)
            with e.Fori(0, TURNS) as i:
                for u in range(STEPS):
                    wait(e, f"v_f{u}", i)
                    for a in range(ACCS):
                        e.dma_start(fa[u][:, a, :, :], accs[a][rows_of(i, u), :].rearrange("(t p) d -> p t d", p=P))\
                            .then_inc(S_(f"ld_f{u}"), 16)

        def vec_out(e):
            with e.Fori(0, TURNS) as i:
                chains = [Chain(e, f"vo{u}", 4 * i) for u in range(STEPS)]

                def sums(u):
                    ch = chains[u]
                    wait(e, f"ld_f{u}", 16 * ACCS * (i + 1))
                    wait(e, f"v_o{u}", i)
                    ch(e.tensor_tensor(flat(fs[u][:, :, :]), flat(fa[u][:, 2, :, :]), flat(fa[u][:, 3, :, :]), ALU.add))
                    wait(e, f"g_fa{u}", i + 1)
                    e.tensor_tensor(flat(fs[u][:, :, :]), flat(fs[u][:, :, :]), flat(fa[u][:, 0, :, :]), ALU.add)\
                        .then_inc(S_(f"v_f{u}"), 1)
                    wait(e, f"v_f{u}", i + 1)
                    for t in range(FT):
                        m = e.bn_stats(fst[u][:, t, :], fs[u][:, t, :])
                    ch(m, alone=True)
                    for t in range(FT):
                        m = e.bn_aggr(fag[u][:, t, :], fst[u][:, t, :])
                    ch(m)
                    ch(e.tensor_scalar(fve[u][:, :], fag[u][:, :, 1], LN_EPS, None, ALU.add))
                    e.tensor_copy(fmean[u][:, :], fag[u][:, :, 0]).then_inc(S_(f"v_fve{u}"), 1)

                def norm(u):
                    wait(e, f"g_f{u}", i + 1)
                    wait(e, f"st_out{u}", 16 * i)
                    for t in range(FT):
                        m = e.tensor_scalar(fo[u][:, t, :], fs[u][:, t, :], fmean[u][:, t:t + 1], frs[u][:, t:t + 1],
                                            ALU.subtract, ALU.mult)
                    m.then_inc(S_(f"v_o{u}"), 1)

                staggered(sums, norm)

        def pool_out(e):
            with e.Fori(0, TURNS) as i:
                def add(u):
                    wait(e, f"ld_f{u}", 16 * ACCS * (i + 1))
                    e.tensor_tensor(flat(fa[u][:, 0, :, :]), flat(fa[u][:, 0, :, :]), flat(fa[u][:, 1, :, :]), ALU.add)\
                        .then_inc(S_(f"g_fa{u}"), 1)

                def power(u):
                    wait(e, f"v_fve{u}", i + 1)
                    e.tensor_tensor(frs[u][:, :], fve[u][:, :], fhalf[:, :], ALU.pow).then_inc(S_(f"g_f{u}"), 1)

                staggered(add, power)

        def act_out(e):
            with e.Fori(0, TURNS) as i:
                for u in range(STEPS):
                    wait(e, f"v_o{u}", i + 1)
                    e.dma_start(out[rows_of(i, u), :].rearrange("(t p) d -> p t d", p=P), fo[u][:, :, :])\
                        .then_inc(S_(f"st_out{u}"), 16)
            for u in range(STEPS):
                wait(e, f"st_out{u}", 16 * TURNS)

        @blk.tensor
        def _(e):
            pe_setup(e)

            run_stage_a(e, (
                (CROSS, pe_kv), (SELF, pe_z), (CROSS, pe_q), (PLACE, pe_rank), (SELF, pe_scores1), (MIX, pe_x2T),
                (CROSS, pe_scores2), (SELF, pe_vo), (MIX, pe_router), (SELF, pe_prT), (CROSS, pe_pT),
                (SELF, pe_av1), (CROSS, pe_av2), (MIX, pe_shared_in), (SELF, pe_x1T), (CROSS, pe_oT),
                (MIX, pe_hsT), (CROSS, pe_out2), (MIX, pe_shared_out)))
            pe_tables(e)
            wait(e, "ld_we", 16 * nseq)

            first = experts(e, 0)
            pe_xbT(e, 0, 0)
            pe_xbT(e, 0, 1)
            pe_gu(e, 0, 0, first[0])
            pe_xbT(e, 0, 2)
            pe_gu(e, 0, 1, first[1])
            pe_xbT(e, 0, 3)
            pe_gu(e, 0, 2, first[2])
            pe_hbT(e, 0, 0)
            with e.Fori(0, BLOCKS // UNROLL) as turn:
                b = turn
                w = experts(e, turn)
                for u in range(UNROLL):
                    pe_xbT(e, b, u + 4)
                    pe_gu(e, b, u + 3, w[u + 3])
                    pe_hbT(e, b, u + 1)
                    pe_down(e, b, u, w[u])

        def copy(e, o, i, done):
            e.activation(o, i, ACT.Copy).then_inc(S_(done), 1)

        def act_z(e, i):
            wait(e, "p_z", i + 1)
            wait(e, "p_s1", i)
            for k in range(DK):
                m = e.activation(zT[:, k, :], bank[0][:, k * S:(k + 1) * S], ACT.Identity, bias=g_bias[:, k, 0:1])
            m.then_inc(S_("a_z"), 1)

        def act_kv(e, i):
            wait(e, "p_k", i + 1)
            wait(e, "p_s2", i)
            for k in range(DK):
                for hh in range(2):
                    places = slice(0, 4, 3) if hh == 0 else slice(1, 3)
                    m = e.activation(
                        kM[:, k, :, :, :].rearrange("p (t a) h c -> p t (a h) c", a=2)[:, :, places, :],
                        bank[2][:, k * S:(k + 1) * S].rearrange("p (t a c) -> p t a c", a=2, c=CH),
                        ACT.Identity, scale=c("headmask")[:, hh:hh + 1], bias=bk_masked[:, k, hh:hh + 1])
            m.then_inc(S_("a_k"), 1)
            wait(e, "p_v", i + 1)
            wait(e, "p_av2", 2 * i)
            for t in range(T):
                for hh in range(2):
                    for a in range(2):
                        rows = slice((a ^ hh) * CH, ((a ^ hh) + 1) * CH)
                        at = (2 * a + hh) * HD
                        m = e.activation(vM[rows, t, :, at:at + HD],
                                         bank[3 + t][rows, hh * P:(hh + 1) * P].rearrange("p (n d) -> p n d", d=HD),
                                         ACT.Copy)
            m.then_inc(S_("a_v"), 1)

        def act_vo(e, i):
            wait(e, "p_vo", i + 1)
            wait(e, "p_av1", i)
            copy(e, vo[:, :, :].rearrange("p t d -> p (t d)"), bank[0][:, :], "a_vo")

        def act_tanh(e, i):
            wait(e, "p_s1", i + 1)
            wait(e, "v_th", i)
            for t in range(T):
                e.activation(t1[:, t, :], bank[1][:, t * S:(t + 1) * S], ACT.Tanh, scale=0.5, bias=r_half[:, t:t + 1])
                m = e.activation(t2[:, t, :], bank[1][:, t * S:(t + 1) * S], ACT.Tanh, bias=r_sb[:, t:t + 1])
            m.then_inc(S_("a_tanh"), 1)

        def act_pr(e, i):
            wait(e, "v_mx", i + 1)
            wait(e, "p_prT", i)
            for t in range(T):
                m = e.activation(pr[:, t, :], th[:, t, :], ACT.Exp, scale=0.1, bias=nmx[:, t:t + 1],
                                 accum_out=den[:, t:t + 1])
            m.then_inc(S_("a_pr"), 1)

        def act_prT(e, i):
            wait(e, "p_prT", i + 1)
            wait(e, "p_av1", i)
            copy(e, prT[:, :, :, :].rearrange("p a b c -> p (a b c)"), bank[0][:, :], "a_prT")

        def act_q(e, i):
            wait(e, "p_q", i + 1)
            wait(e, "p_s2", i)
            for k in range(DK):
                m = e.activation(qT[:, k, :], bank[5][:, k * S:(k + 1) * S], ACT.Identity,
                                 bias=b_cross[:, k, 0:1])
            m.then_inc(S_("a_q"), 1)

        def act_sh(e, i):
            for t in range(T):
                wait(e, "v_sh", T * i + t + 1)
                e.activation(sh[:, :, t, :], sh[:, :, t, :], ACT.Exp, scale=HD ** -0.5).then_inc(S_("a_sh"), 1)

        def act_pT(e, i):
            for t in range(T):
                wait(e, "p_pT", 4 * i + 2 * t + 1)
                wait(e, "p_av2", 2 * i)
                copy(e, pT[:, t, 0:4, :].rearrange("p a b -> p (a b)"), bank[2 + 2 * t][:, :], "a_pT")

        def act_oT(e, i):
            wait(e, "p_oT", i + 1)
            wait(e, "p_out2", i)
            copy(e, oT[:, :, :].rearrange("p a b -> p (a b)"), bank[3][:, :], "a_oT")

        def act_x2T(e, i):
            wait(e, "p_x2T", i + 1)
            wait(e, "p_shin", T * i)
            copy(e, x2T[:, :, :].rearrange("p a b -> p (a b)"), bank[6][:, :], "a_x2T")

        def act_sc(e, i):
            wait(e, "p_router", i + 1)
            wait(e, "v_msel", i)
            e.activation(sc[:, :, :].rearrange("p a b -> p (a b)"), bank[7][:, 0:T * E], ACT.Tanh, scale=0.5)\
                .then_inc(S_("a_sc"), 1)

        def act_gates(e, i):
            wait(e, "p_hsT", i)
            for t in range(T):
                wait(e, "p_shin", T * i + t + 1)
                m = e.activation(hs[:, t, :], bank[6 + t][:, 0:SH], ACT.Tanh, scale=0.5)
            m.then_inc(S_("a_hg"), 1)

        def act_hsT(e, i):
            wait(e, "p_hsT", i + 1)
            wait(e, "p_shout", i)
            copy(e, hsT[:, :, :].rearrange("p a b -> p (a b)"), bank[6][:, :], "a_hsT")

        def act_xbT(e, b, u):
            n = number(b, u)
            wait(e, "p_xbT", n + 1)
            wait(e, "p_gu", n - 1)
            copy(e, xbT[u % 2][:, :], bank[u % 2][:, 0:D], "a_xbT")

        def act_gb(e, b, u):
            n = number(b, u)
            wait(e, "p_gu", n + 1)
            wait(e, "v_hb", n - 1)
            e.activation(gb[u % 2][:, :], bank[2 + u % 2][:, 0:EI], ACT.Tanh, scale=0.5).then_inc(S_("a_gb"), 1)

        def act_yb(e, b, u):
            n = number(b, u)
            wait(e, "p_down", n + 1)
            wait(e, "v_taken", n + 1)
            wait(e, f"st_acc{u % ACCS}", 16 * adds_before(b, u))
            e.activation(yb[u % ACCS][:, :], bank[6 + u % 2][:, 0:D], ACT.Copy, scale=wcol[u % UNROLL][:, 0:1])\
                .then_inc(S_("a_yb"), 1)

        @blk.scalar
        def _(e):
            wait(e, "v_setup", 1)

            run_stage_a(e, (
                (CROSS, act_kv), (SELF, act_z), (CROSS, act_q), (MIX, act_x2T), (SELF, act_tanh), (SELF, act_vo),
                (SELF, act_pr), (MIX, act_sc), (CROSS, act_sh), (SELF, act_prT), (CROSS, act_pT), (MIX, act_gates),
                (CROSS, act_oT), (MIX, act_hsT)))
            pad_rows(e, E // 2, E)
            wait(e, "v_tab", 1)
            act_xbT(e, 0, 0)
            act_xbT(e, 0, 1)
            act_gb(e, 0, 0)
            act_xbT(e, 0, 2)
            act_gb(e, 0, 1)
            act_xbT(e, 0, 3)
            act_gb(e, 0, 2)
            with e.Fori(0, BLOCKS // UNROLL) as turn:
                b = turn
                for u in range(UNROLL):
                    act_xbT(e, b, u + 4)
                    act_gb(e, b, u + 3)
                    act_yb(e, b, u)
            act_out(e)

        NR = {"v1": 5, "v2": 4, "v3": 21, "v4": 4}

        def vec_r(e, i, ch):
            wait(e, "p_r", i + 1)
            wait(e, "a_tanh", i)
            ch(e.tensor_scalar(r_sb[:, :], bank[1][:, 0:T], c_bqbk[:, 0:1], None, ALU.add))
            e.tensor_scalar(r_half[:, :], r_sb[:, :], 0.5, None, ALU.mult)
            e.tensor_scalar(r_neg[:, :], r_sb[:, :], -1.0, None, ALU.mult).then_inc(S_("v_r"), 1)

        def vec_th(e, i, ch):
            wait(e, "v_r", i + 1)
            wait(e, "a_tanh", i + 1)
            wait(e, "a_pr", i)
            for t in range(T):
                m = e.scalar_tensor_tensor(th[:, t, :], bank[1][:, t * S:(t + 1) * S], r_neg[:, t:t + 1],
                                           t1[:, t, :], ALU.max, ALU.add)
            ch(m)
            f = lambda a: a[:, :, :].rearrange("p a b -> p (a b)")
            e.scalar_tensor_tensor(f(th), f(t2), 1.5, f(th), ALU.mult, ALU.add).then_inc(S_("v_th"), 1)
            wait(e, "v_th", i + 1)
            ch(e.tensor_reduce(mx[:, :], th[:, :, :], AX.X, ALU.max))
            e.tensor_scalar(nmx[:, :], mx[:, :], -0.1, None, ALU.mult).then_inc(S_("v_mx"), 1)

        def stats(e, ch, stats, aggr, ve, told, src):
            for t in range(T):
                m = e.bn_stats(stats[:, t, :], src[:, t, :])
            ch(m, alone=True)
            for t in range(T):
                m = e.bn_aggr(aggr[:, t, :], stats[:, t, :])
            ch(m)
            e.tensor_scalar(ve[:, :], aggr[:, :, 1], LN_EPS, None, ALU.add).then_inc(S_(told), 1)

        def normalize(e, src, aggr, rs, dst, done):
            for t in range(T):
                m = e.tensor_scalar(dst[:, t, :], src[:, t, :], aggr[:, t, 0:1], rs[:, t:t + 1],
                                    ALU.subtract, ALU.mult)
            m.then_inc(S_(done), 1)

        def vec_x1(e, i, ch):
            wait(e, "p_av1", i + 1)
            wait(e, "a_pr", i + 1)
            wait(e, "g_xc", i + 1)
            e.reciprocal(den[:, :], den[:, :]).then_inc(S_("v_rd"), 1)
            wait(e, "v_rd", i + 1)
            for t in range(T):
                m = e.scalar_tensor_tensor(xc[:, t, :], bank[1][:, t * D:(t + 1) * D], den[:, t:t + 1],
                                           xc[:, t, :], ALU.mult, ALU.add)
            m.then_inc(S_("v_pre1"), 1)
            wait(e, "v_pre1", i + 1)
            stats(e, ch, st1, ag1, ve1, "v_ve1", xc)

        def vec_norm1(e, i, ch):
            wait(e, "g_rs1", i + 1)
            wait(e, "p_x1T", i)
            wait(e, "g_xc2", i)
            normalize(e, xc, ag1, rs1, x1, "v_x1")

        def vec_x1T(e, i, ch):
            wait(e, "p_x1T", i + 1)
            wait(e, "p_q", i)
            e.tensor_copy(x1T[:, :, :].rearrange("p a b -> p (a b)"), bank[0][:, :]).then_inc(S_("v_x1T"), 1)

        def vec_sh(e, i, ch):
            wait(e, "p_pT", 4 * i)
            wait(e, "p_s2", i + 1)
            for t in range(T):
                cols = slice(t * 4 * CH, (t + 1) * 4 * CH)
                for j in range(4):
                    m = e.tensor_reduce(mxh[:, j, t, :, :].rearrange("p b c -> p (b c)"),
                                        bank[2 + j][:, cols].rearrange("p (a b) -> p a b", b=CH), AX.X, ALU.max)
                m.then_inc(S_("v_mxh"), 1)
                wait(e, "v_mxh", T * i + t + 1)
                for j in range(4):
                    most = mxh[:, j, t, :, :].rearrange("p b (c o) -> p (b c) o", o=1).to_broadcast([P, 4, CH])
                    m = e.tensor_tensor(sh[:, j, t, :].rearrange("p (b c) -> p b c", c=CH),
                                        bank[2 + j][:, cols].rearrange("p (a b) -> p a b", b=CH), most, ALU.subtract)
                m.then_inc(S_("v_sh"), 1)

        def vec_pT(e, i, ch):
            for t in range(T):
                wait(e, "p_pT", 4 * i + 2 * t + 2)
                wait(e, "p_av2", 2 * i)
                e.tensor_copy(pT[:, t, 4:8, :].rearrange("p a b -> p (a b)"), bank[3 + 2 * t][:, :])\
                    .then_inc(S_("v_pT"), 1)

        def vec_o(e, i, ch):
            for t in range(T):
                wait(e, "p_av2", 2 * i + t + 1)
                if t == 0:
                    wait(e, "p_oT", i)
                av = [bank[2 + 2 * t + g][:, 0:4 * VW].rearrange("p (n w) -> p n w", w=VW) for g in range(2)]
                for g in range(2):
                    m = e.reciprocal(rden[:, t, 4 * g:4 * g + 4, :], av[g][:, :, 4 * HD:VW])
                ch(m)
                for g in range(2):
                    for a in range(2):
                        rows = slice(a * CH, (a + 1) * CH)
                        m = e.tensor_tensor(
                            o_sb[rows, t, g * P:(g + 1) * P].rearrange("p (n h d) -> p n h d", n=4, h=2),
                            av[g][rows, :, a * 2 * HD:(a + 1) * 2 * HD].rearrange("p n (h d) -> p n h d", h=2),
                            rden[rows, t, 4 * g:4 * g + 4, 2 * a:2 * a + 2].rearrange("p n (h o) -> p n h o", o=1)
                            .to_broadcast([CH, 4, 2, HD]), ALU.mult)
            m.then_inc(S_("v_o"), 1)

        def vec_x2(e, i, ch):
            wait(e, "p_out2", i + 1)
            wait(e, "g_xc2", i + 1)
            f = lambda a: a[:, :, :].rearrange("p a b -> p (a b)")
            e.tensor_tensor(f(xc2), bank[5][:, :], f(xc2), ALU.add).then_inc(S_("v_pre2"), 1)
            wait(e, "v_pre2", i + 1)
            stats(e, ch, st2, ag2, ve2, "v_ve2", xc2)

        def vec_norm2(e, i, ch):
            wait(e, "g_rs2", i + 1)
            wait(e, "p_x2T", i)
            wait(e, "g_row", i)
            normalize(e, xc2, ag2, rs2, x2, "v_x2")

        def vec_route(e, i, ch):
            wait(e, "a_sc", i + 1)
            ch(e.tensor_scalar(sc[:, :, :], sc[:, :, :], 0.5, 0.5, ALU.mult, ALU.add))
            rb = bias_router[:, :].rearrange("p (a b) -> p a b", a=1).to_broadcast([P, T, E])
            ch(e.tensor_tensor(sfc[:, :, :], sc[:, :, :], rb, ALU.add), alone=True)
            for t in range(T):
                for g in range(GRP):
                    m = e.max(g8[:, t, g, :], sfc[:, t, g * GE:(g + 1) * GE])
            ch(m)
            ch(e.tensor_tensor(gs[:, :, 0:GRP], g8[:, :, :, 0], g8[:, :, :, 1], ALU.add), alone=True)
            for t in range(T):
                m = e.max(gm[:, t, :], gs[:, t, :])
            ch(m)
            ch(e.tensor_copy(gv[:, :, 0:TOPG], gm[:, :, 0:TOPG]), alone=True)
            for t in range(T):
                m = e.match_replace(gr[:, t, :], gv[:, t, :], gs[:, t, :], BIG)
            ch(m)
            ch(e.tensor_scalar(gsel[:, :, :], gr[:, :, 0:GRP], BIG, None, ALU.is_ge))
            for t in range(T):
                m = e.tensor_tensor(tmp[:, t, 0:E].rearrange("p (a b) -> p a b", a=GRP),
                                    sfc[:, t, :].rearrange("p (a b) -> p a b", a=GRP),
                                    gsel[:, t, :].rearrange("p (a b) -> p a b", b=1).to_broadcast([P, GRP, GE]),
                                    ALU.mult)
            ch(m)
            ch(e.tensor_scalar(tmp[:, :, 0:E], tmp[:, :, 0:E], 0.0, None, ALU.add), alone=True)
            for t in range(T):
                m = e.max(em[:, t, :], tmp[:, t, 0:E])
            ch(m)
            ch(e.tensor_copy(ev[:, :, 0:TOPK], em[:, :, 0:TOPK]), alone=True)
            for t in range(T):
                m = e.match_replace(er[:, t, :], ev[:, t, :], tmp[:, t, :], BIG)
            ch(m)

        def vec_choice(e, i, ch):
            wait(e, "p_rank", i)
            ch(e.tensor_scalar(msel[:, :, :], er[:, :, 0:E], BIG, None, ALU.is_ge))
            for t in range(1, T):
                ch(e.tensor_tensor(macc[:, t, :], macc[:, t - 1, :], msel[:, t - 1, :], ALU.add))
            ch(e.tensor_tensor(wraw[:, :, :], sc[:, :, :], msel[:, :, :], ALU.mult))
            ch(e.tensor_reduce(wsum[:, :], wraw[:, :, :], AX.X, ALU.add))
            ch(e.tensor_scalar(wsum[:, :], wsum[:, :], 1e-20, None, ALU.add))
            ch(e.reciprocal(wsum[:, :], wsum[:, :]))
            wait(e, "g_row", i + 1)
            for t in range(T):
                m = e.tensor_scalar(row[:, t, D:D + E], wraw[:, t, :], wsum[:, t:t + 1], 0.5 * ROUTE_SCALE,
                                    ALU.mult, ALU.mult)
            ch(m)
            m = e.tensor_scalar(row[:, :, D + E].bitcast(I32), row[:, :, D + E].bitcast(I32), float(S), None, ALU.add)
            m.then_inc(S_("v_msel"), 1)

        def vec_hs(e, i, ch):
            wait(e, "a_hg", i + 1)
            for t in range(T):
                m = e.scalar_tensor_tensor(hs[:, t, :], hs[:, t, :], 1.0, bank[6 + t][:, 0:SH], ALU.add, ALU.mult)
            ch(m)
            for t in range(T):
                m = e.tensor_tensor(hs[:, t, :], hs[:, t, :], bank[6 + t][:, SH:2 * SH], ALU.mult)
            m.then_inc(S_("v_hs"), 1)

        def vec_key(e, i, ch):
            wait(e, "p_rank", i + 1)
            rank = bank[6][:, 0:T * E].rearrange("p (a b) -> p a b", a=T)
            start = c("region").rearrange("p (a b) -> p a b", a=1).to_broadcast([P, T, E])
            ch(e.tensor_tensor(key[:, :, :], rank, start, ALU.add))
            ch(e.tensor_tensor(macc[:, 0, :], macc[:, T - 1, :], msel[:, T - 1, :], ALU.add))
            ch(e.tensor_tensor(key[:, :, :], key[:, :, :], msel[:, :, :], ALU.mult), alone=True)
            for t in range(T):
                m = e.max(slot[:, t, :], key[:, t, :])
            ch(m)
            wait(e, "st_row", 16 * TOPK * T * i)
            e.tensor_scalar(idx[:, :, :], slot[:, :, 0:TOPK], -1.0, None, ALU.add).then_inc(S_("v_key"), 1)

        def vec_acc(e, i, ch):
            wait(e, "p_shout", i + 1)
            wait(e, "st_acc", 16 * i)
            for t in range(T):
                m = e.scalar_tensor_tensor(acc_sb[:, t, :], bank[7][:, t * D:(t + 1) * D], 0.5, row[:, t, 0:D],
                                           ALU.mult, ALU.add)
            m.then_inc(S_("v_acc"), 1)

        def vec_tables(e):
            ch = Chain(e, "vt", 0)
            wait(e, "p_tab", 1)
            ch(e.tensor_scalar(counts[:, :], bank[7][0:E, 0:1], float(P - 1), None, ALU.add))
            ch(e.tensor_tensor(padrow[:, :], bank[7][0:1, 32:32 + E], c("region", 1), ALU.add))
            e.tensor_scalar(padrow[:, :], padrow[:, :], -1.0, None, ALU.add).then_inc(S_("v_padrow"), 1)
            ch(e.tensor_copy(cnt_i[:, :], counts[:, :]))
            ch(e.tensor_scalar(cnt_i[:, :], cnt_i[:, :], 7, None, ALU.logical_shift_right))
            e.tensor_copy(nblk[:, :], cnt_i[:, :]).then_inc(S_("v_nblk"), 1)
            wait(e, "p_tab", 2)
            ch(e.tensor_copy(upto[:, :], bank[7][0:E, 1:2]))
            e.tensor_scalar(past[:, :], c("blockno", E), upto[:, 0:1], None, ALU.is_ge).then_inc(S_("v_past"), 1)
            wait(e, "p_tab", 3)
            ch(e.tensor_tensor(tab[:, 0, :], c("blockno", 1), bank[6][0:1, TABLE:2 * TABLE], ALU.subtract))
            ch(e.tensor_scalar(tab[:, 0, :], tab[:, 0, :], float(P), None, ALU.mult))
            ch(e.tensor_scalar(tab[:, 1, :], bank[6][0:1, 0:TABLE], float(REGION), None, ALU.mult))
            ch(e.tensor_tensor(tab[:, 0, :], tab[:, 0, :], tab[:, 1, :], ALU.add))
            ch(e.tensor_scalar(tab_i[:, 0, :], tab[:, 0, :], float(E * REGION), None, ALU.min))
            ch(e.tensor_scalar(tab[:, 1, :], bank[6][0:1, 0:TABLE], float(E - 1), None, ALU.min))
            ch(e.tensor_copy(tab_i[:, 1, :], tab[:, 1, :]))
            for j in range(2):
                for v in reversed(range(WORD)):
                    at = j * WORD + v
                    x = tab_i[:, 1, at:at + BLOCKS - UNROLL + 1:UNROLL]
                    if v == WORD - 1:
                        ch(e.tensor_copy(words[:, :, j], x))
                    else:
                        ch(e.tensor_scalar(words[:, :, j], words[:, :, j], 5, None, ALU.logical_shift_left))
                        ch(e.tensor_tensor(words[:, :, j], words[:, :, j], x, ALU.bitwise_or))
            e.nop().then_inc(S_("v_tab"), 1)

        def vec_hb(e, b, u):
            n = number(b, u)
            wait(e, "a_gb", n + 1)
            e.scalar_tensor_tensor(hb1[u % 2][:, :], gb[u % 2][:, :], 1.0, bank[2 + u % 2][:, 0:EI],
                                   ALU.add, ALU.mult).then_inc(S_("v_hb1"), 1)
            wait(e, "v_hb1", n + 1)
            wait(e, "p_hbT", n - 1)
            e.tensor_tensor(hb[u % 2][:, :], hb1[u % 2][:, :], bank[2 + u % 2][:, EI:2 * EI], ALU.mult)\
                .then_inc(S_("v_hb"), 1)

        def vec_taken(e, b, u, x):
            n = number(b, u)
            wait(e, f"ld_row{u % UNROLL}", 16 * loads_of_buffer(b, u))
            if not isinstance(n, int):
                wait(e, "a_yb", n - UNROLL + ACCS + 1)
            v = u % UNROLL
            e.tensor_copy(wcol[v][:, :], rowsb[v][:, bass.ds(x + D, 1)])
            e.tensor_copy(idcol[v][:, :], rowsb[v][:, D + E:RW].bitcast(I32)).then_inc(S_("v_taken"), 1)

        def vec_hbT(e, b, u):
            n = number(b, u)
            wait(e, "p_hbT", n + 1)
            wait(e, "p_down", n - 1)
            e.tensor_copy(hbT[u % 2][:, :], bank[4 + u % 2][:, 0:EI]).then_inc(S_("v_hbT"), 1)

        @blk.vector
        def _(e):
            ch = Chain(e, "vs", 0)
            e.memset(half_neg[:, :], -0.5).then_inc(S_("v_const"), 1)
            e.memset(fhalf[:, :], -0.5)
            e.memset(gs[:, :, :], -BIG)
            e.memset(gv[:, :, :], -BIG)
            e.memset(tmp[:, :, :], -BIG)
            e.memset(ev[:, :, :], -BIG)
            e.memset(pad[:, :], 0.0)
            e.memset(vM[:, :, :, :], 0.0)
            ch(e.memset(macc[:, :, :], 0.0))
            wait(e, "g_iota", 2)
            e.tensor_copy(pad[:, D + E:RW].bitcast(I32), pad_id[:, :]).then_inc(S_("v_pad"), 1)
            ch(e.tensor_copy(row[:, :, D + E].bitcast(I32), tok_id[:, :]))
            wait(e, "ld_const", 16 * 7)
            for t in range(T):
                e.tensor_copy(vM[:, t, :, 4 * HD:4 * HD + 2], c("valmask").rearrange(
                    "p (a b) -> p a b", a=1).to_broadcast([P, NP, 2]))
                for h in range(2):
                    at = 4 * HD + 2 + h
                    m = e.tensor_copy(vM[:, t, :, at:at + 1], c("valmask")[:, 1 - h:2 - h].rearrange(
                        "p (a b) -> p a b", a=1).to_broadcast([P, NP, 1]))
            for k in range(DK):
                for hh in range(2):
                    e.tensor_scalar(bk_masked[:, k, hh:hh + 1], c("headmask")[:, hh:hh + 1], b_cross[:, k, 1:2], None,
                                    ALU.mult)
            for k in range(DK):
                for j, b in enumerate((b_attn[:, k, 0:1], b_attn[:, k, 2:3], b_attn[:, k, 3:4])):
                    m = e.tensor_scalar(rep[:, k, j, :], c("ones"), b, None, ALU.mult)
            m.then_inc(S_("v_rep"), 1)
            wait(e, "p_setup", 1)
            e.tensor_copy(g_qk[:, :, :].rearrange("p a b -> p (a b)"), bank[0][:, :])
            e.tensor_copy(g_vo[:, :, :].rearrange("p a b -> p (a b)"), bank[1][:, :])
            e.tensor_copy(g_bias[:, :, :], bank[2][:, 0:4].rearrange("p (j k) -> p k j", j=2))
            e.tensor_copy(c_bqbk[:, :], bank[2][:, 8:9])
            e.tensor_copy(c_out[:, :, :].rearrange("p a b -> p (a b)"), bank[3][:, :]).then_inc(S_("v_setup"), 1)

            def chains(seqs):
                return [None if i is None else Chain(e, n, NR[n] * i) for n, i in zip(NR, seqs)]

            def closed(chs):
                for ch in chs:
                    assert ch is None or ch.n == NR[ch.name], (ch.name, ch.n)

            run_stage_a(e, (
                (SELF, vec_r), (PLACE, vec_key), (SELF, vec_th), (CROSS, vec_sh), (MIX, vec_route),
                (CROSS, vec_pT), (SELF, vec_x1), (CROSS, vec_o), (SELF, vec_norm1), (MIX, vec_hs),
                (MIX, vec_choice), (SELF, vec_x1T), (CROSS, vec_x2), (MIX, vec_acc), (CROSS, vec_norm2)),
                chains, closed)
            vec_tables(e)

            wait(e, "v_tab", 1)

            x = experts(e, 0)
            for u in range(2):
                vec_taken(e, 0, u, x[u])
            vec_hb(e, 0, 0)
            vec_hb(e, 0, 1)
            vec_hbT(e, 0, 0)
            with e.Fori(0, BLOCKS // UNROLL) as turn:
                b = turn
                x = experts(e, turn)
                for u in range(UNROLL):
                    vec_hb(e, b, u + 2)
                    vec_hbT(e, b, u + 1)
                    vec_taken(e, b, u + 2, x[u + 2])
            vec_out(e)

        def pool_xc(e, i):
            wait(e, "ld_x", 16 * (i + 1))
            wait(e, "v_x1", i)
            for t in range(T):
                m = e.tensor_tensor(xc[:, t, :], x_sb[:, t, :], c_out[:, 0, :], ALU.add)
            m.then_inc(S_("g_xc"), 1)

        def pool_rs1(e, i):
            wait(e, "v_ve1", i + 1)
            e.tensor_tensor(rs1[:, :], ve1[:, :], half_neg[:, :], ALU.pow).then_inc(S_("g_rs1"), 1)

        def pool_rs2(e, i):
            wait(e, "v_ve2", i + 1)
            e.tensor_tensor(rs2[:, :], ve2[:, :], half_neg[:, :], ALU.pow).then_inc(S_("g_rs2"), 1)

        def pool_row(e, i):
            wait(e, "v_x2", i + 1)
            wait_apart(e, ("v_acc", i),
                       ("st_row", 16 * TOPK * T * i))
            e.tensor_copy(row[:, :, 0:D], x2[:, :, :]).then_inc(S_("g_row"), 1)

        def pool_xc2(e, i):
            wait(e, "v_x1", i + 1)
            wait(e, "v_x2", i)
            for t in range(T):
                m = e.tensor_tensor(xc2[:, t, :], x1[:, t, :], c_out[:, 1, :], ALU.add)
            m.then_inc(S_("g_xc2"), 1)

        def pool_scatter(e, i):
            wait_apart(e, ("v_key", i + 1),
                       ("v_msel", i + 1))
            for t in range(T):
                for k in range(TOPK):
                    e.indirect_dma_start(routed, bass.IndirectOffsetOnAxis(ap=idx[:, t, k:k + 1], axis=0),
                                         row[:, t, :], None).then_inc(S_("st_row"), 16)

        @blk.gpsimd
        def _(e):
            for name in LOOKED_BACK:
                e.nop().then_inc(S_(name), FIRST)
            e.iota(pad_id[:, :], [[0, 1]], base=N, channel_multiplier=1).then_inc(S_("g_iota"), 1)
            e.iota(tok_id[:, :], [[P, T]], base=-S, channel_multiplier=1).then_inc(S_("g_iota"), 1)
            wait(e, "v_pad", 1)
            for a in range(ACCS):
                e.dma_start(accs[a][N:N + P, :], pad[:, 0:D]).then_inc(S_(f"st_acc{a}"), 16)
            e.dma_start(routed[E * REGION:E * REGION + P, :], pad[:, :]).then_inc(S_("st_row"), 16)
            wait(e, "v_setup", 1)
            wait(e, "v_const", 1)
            run_stage_a(e, (
                (PLACE, pool_scatter), (MIX, pool_row), (SELF, pool_xc), (SELF, pool_rs1), (CROSS, pool_rs2),
                (SELF, pool_xc2)))
            wait(e, "st_acc", 16 * nseq)
            wait(e, "st_zero", 16 * nseq * (ACCS - 1))
            with e.Fori(0, BLOCKS // UNROLL) as turn:
                b = turn
                for u in range(UNROLL):
                    n = number(b, u)
                    wait_apart(e, ("a_yb", n + 1),
                               (f"st_acc{u % ACCS}", 16 * adds_before(b, u)))
                    e.indirect_dma_start(
                        accs[u % ACCS], bass.IndirectOffsetOnAxis(ap=idcol[u][:, :], axis=0),
                        yb[u % ACCS][:, :], None, compute_op=ALU.add).then_inc(S_(f"st_acc{u % ACCS}"), 16)
            pool_out(e)

        @blk.sync
        def _(e):
            e.dma_start(const[:, :], d["const"]).then_inc(S_("ld_const"), 16)
            e.dma_start(w_attn[:, :, :, :], d["w_attn"]).then_inc(S_("ld_const"), 16)
            e.dma_start(b_attn[:, :, :], d["b_attn"]).then_inc(S_("ld_const"), 16)
            e.dma_start(b_cross[:, :, :], d["b_cross"]).then_inc(S_("ld_const"), 16)
            e.dma_start(bo_rows[:, :, :], d["bo_rows"]).then_inc(S_("ld_const"), 16)
            e.dma_start(w_cross[:, :, :, :], d["w_cross"]).then_inc(S_("ld_const"), 16)
            e.dma_start(bias_router[:, :], d["bias_router"]).then_inc(S_("ld_const"), 16)

            def load_x(e, i):
                wait_apart(e, ("p_vo", i), ("p_s1", i), ("p_r", i))
                e.dma_start(xT[:, :, :], d["xT"][bass.ds(i, 1), :, :].rearrange("a p (k s) -> p (a k) s", k=DK))\
                    .then_inc(S_("ld_xT"), 16)
                wait(e, "g_xc", i)
                e.dma_start(x_sb[:, :, :], d["x"][bass.ds(i, 1), :, :].rearrange("a (t p) d -> p (a t) d", p=P))\
                    .then_inc(S_("ld_x"), 16)

            def load_c(e, i):
                wait(e, "p_v", i)
                e.dma_start(cT[:, :, :, :, :].rearrange("p k t a s -> p (k t a s)"),
                            d["ctxT"][bass.ds(i, 1), :, :].rearrange("a p s -> p (a s)"))\
                    .then_inc(S_("ld_cT"), 16)

            def store_acc(e, i):
                wait(e, "v_acc", i + 1)
                e.dma_start(accs[0][bass.ds(i * S, S), :].rearrange("(t p) d -> p t d", p=P), acc_sb[:, :, :])\
                    .then_inc(S_("st_acc"), 16)

            def load_rest(e, i):
                for a in range(1, ACCS):
                    e.dma_start(accs[a][bass.ds(i * S, S), :].rearrange("(t p) d -> p t d", p=P),
                                pad[:, 0:D].rearrange("p (a d) -> p a d", a=1).to_broadcast([P, T, D]))\
                        .then_inc(S_("st_zero"), 16)
                share = E // nseq * 3 * D
                e.dma_start(w_flat[:, bass.ds(i * share, share)],
                            d["w_expert"].rearrange("p e n -> p (e n)")[:, bass.ds(i * share, share)])\
                    .then_inc(S_("ld_we"), 16)

            e.dma_start(w_router[:, :, :], d["w_router"]).then_inc(S_("ld_w"), 16)
            e.dma_start(w_shared_in[:, :, :], d["w_shared_in"]).then_inc(S_("ld_w"), 16)
            e.dma_start(w_shared_out[:, :, :], d["w_shared_out"]).then_inc(S_("ld_w"), 16)
            wait(e, "v_pad", 1)
            run_stage_a(e, ((PLACE, store_acc), (SELF, load_x), (SELF, load_c), (CROSS, load_rest)))
            pad_rows(e, 0, E // 2)
            wait(e, "v_tab", 1)
            wait(e, "st_row", 16 * TOPK * T * nseq)
            wait(e, "st_acc", 16 * nseq)
            wait(e, "st_pad", 16 * E)

            def load_rows(turn, u):
                at = e.value_load(tab_i[0:1, 0, bass.ds(number(turn, u), 1)], min_val=0, max_val=E * REGION)
                if not isinstance(turn, int):
                    wait_apart(e, ("p_xbT", number(turn, u) - UNROLL + 1), ("v_taken", number(turn, u) - UNROLL + 1))
                e.dma_start(rowsb[u][:, :], routed[bass.ds(at, P), :]).then_inc(S_(f"ld_row{u}"), 16)

            for u in range(UNROLL):
                load_rows(0, u)
            with e.Fori(1, TABLE // UNROLL) as turn:
                for u in range(UNROLL):
                    load_rows(turn, u)
            sync_out(e)



_SHARED = ("w_attn", "b_attn", "b_cross", "bo_rows", "w_cross", "bias_router", "w_router", "w_shared_in",
           "w_shared_out", "w_expert")


def layouts(i):
    f = lambda n: np.asarray(i[n])
    rows = lambda w: w.reshape(DK, P, *w.shape[1:]).swapaxes(0, 1)
    x, ctx = f("x"), f("ctx_1024")
    cols = lambda a: a.transpose(0, 2, 1).reshape(-1, DK, P, S).transpose(0, 2, 1, 3).reshape(-1, P, DK * S)
    ip, ib = f("L0_xattn_in_proj_w"), f("L0_xattn_in_proj_b")
    gu = np.concatenate([f("L0_ffn_gate_w"), f("L0_ffn_up_w")], axis=1)
    gu = gu.transpose(2, 0, 1).reshape(DK, P, E, 2 * EI).transpose(1, 2, 0, 3).reshape(P, E, 2 * D)
    return {
        "x": x,
        "xT": cols(x),
        "ctxT": cols(ctx).reshape(-1, P, DK * T, 2, CH)[:, :, :, [0, 1, 0], :].reshape(-1, P, 3 * DK * T * CH),
        "w_attn": np.stack([rows(f("L0_attn_Wq")), rows(f("L0_attn_Wk")), rows(f("L0_attn_Wv")),
                            rows(f("L0_attn_Wo").T)], axis=2),
        "b_attn": np.stack([rows(f("L0_attn_bq")), rows(f("L0_attn_bk")), rows(f("L0_attn_bv")),
                            rows(ib[2 * D:])], axis=2),
        "b_cross": np.stack([rows(ib[:D]), rows(ib[D:2 * D])], axis=2),
        "bo_rows": np.stack([f("L0_attn_bo"), f("L0_xattn_out_proj_b")])[None],
        "w_cross": np.stack([rows(ip[:D].T), rows(ip[D:2 * D].T), rows(ip[2 * D:].T),
                             rows(f("L0_xattn_out_proj_w").T)], axis=2),
        "bias_router": np.tile(f("L0_ffn_router_bias"), (P, 1)),
        "w_router": rows(f("L0_ffn_router_weight").T),
        "w_shared_in": rows(np.concatenate([f("L0_ffn_shared_gate_w"), f("L0_ffn_shared_up_w")], axis=0).T),
        "w_shared_out": rows(f("L0_ffn_shared_down_w").T),
        "w_expert": np.concatenate([gu, f("L0_ffn_down_w").transpose(2, 0, 1)], axis=2),
        "const": constants(x.shape[0])[1],
    }


def kernel(**inputs):
    import concourse.bacc as bacc
    from concourse.bass_utils import run_bass_kernel_spmd

    nc = bacc.Bacc("TRN2", target_bir_lowering=False, num_devices=1)
    arrays = {name: np.ascontiguousarray(a) for name, a in layouts(inputs).items()}
    d = {name: nc.dram_tensor(name, a.shape, mybir.dt.from_np(a.dtype), kind="ExternalInput").ap()
         for name, a in arrays.items()}
    shape = arrays["x"].shape
    out = nc.dram_tensor("out", (shape[0] * S, D), mybir.dt.float32, kind="ExternalOutput").ap()
    build(nc, d, out)
    r = run_bass_kernel_spmd(nc, [arrays], core_ids=[0])
    return r.results[0]["out"].reshape(shape)
```
